# Optimizing a Trainium2 kernel written in Bass

```python
import numpy as np
import jax
import jax.numpy as jnp

def _softmax(x, axis=-1):
    return jax.nn.softmax(x, axis=axis)

def _gelu(x):
    return jax.nn.gelu(x, approximate=True)

def _silu(x):
    return jax.nn.silu(x)

def _sigmoid(x):
    return jax.nn.sigmoid(x)

def _layernorm(x, axis=-1, eps=1e-05):
    m = jnp.mean(x, axis=axis, keepdims=True)
    v = jnp.var(x, axis=axis, keepdims=True)
    return (x - m) / jnp.sqrt(v + eps)

def _scatter_add(tgt, idx, src, axis=0):
    return tgt.at[idx].add(src)

def _segment_sum(src, seg, n):
    return jax.ops.segment_sum(src, seg, n)
kernel_name = 'mk_recurrent_d1_jaxref_r8_259761'

def setup_inputs(seed: int=0):
    np.random.seed(seed)
    _w = jnp.asarray

    def _L0_attn_setup():
        import jax, jax.numpy as jnp
        import numpy as np
        HID = 256
        H = 16
        KVH = 8
        D = HID // H
        WIN = 128
        KEEP = 0.33
        HOPS = 2
        ALPHA = 0.7
        NEG = -10000.0

        def _build_tls_mask(x):
            B, S, _ = x.shape
            norm = jnp.linalg.norm(x, axis=-1)
            mean = jnp.mean(x, axis=1, keepdims=True)
            mnorm = jnp.linalg.norm(mean, axis=-1)
            div = -jnp.sum(x * mean, axis=-1) / (norm * mnorm + 1e-06)
            score = ALPHA * norm + (1.0 - ALPHA) * div
            k = max(1, int(KEEP * S))
            _, idx = jax.lax.top_k(score, k)
            lm = jnp.zeros((B, S), bool).at[jnp.arange(B)[:, None], idx].set(True)
            for _ in range(HOPS):
                lm = lm | jnp.pad(lm[:, :-1], ((0, 0), (1, 0))) | jnp.pad(lm[:, 1:], ((0, 0), (0, 1)))
            i = jnp.arange(S)[:, None]
            j = jnp.arange(S)[None, :]
            causal = j <= i
            local = i - j < WIN
            mask = causal & (local | lm[:, None, :])
            return mask[:, None]
        key = jax.random.key(seed)
        ks = jax.random.split(key, 5)
        B, S = (2, 256)
        s = 0.02
        return {'hidden_states': jax.random.normal(ks[0], (B, S, HID), jnp.float32), 'Wq': jax.random.normal(ks[1], (HID, HID), jnp.float32) * s, 'Wk': jax.random.normal(ks[2], (HID, KVH * D), jnp.float32) * s, 'Wv': jax.random.normal(ks[3], (HID, KVH * D), jnp.float32) * s, 'Wo': jax.random.normal(ks[4], (HID, HID), jnp.float32) * s}
    _L0_attn_in = _L0_attn_setup()

    def _L0_ffn_setup():
        import jax, jax.numpy as jnp
        import numpy as np
        D_MODEL = 256
        D_FF = 1024

        def absmean_quant(w):
            scale = jnp.mean(jnp.abs(w))
            mask = (jnp.abs(w) >= scale * 0.7).astype(w.dtype)
            return jnp.sign(w) * mask
        key = jax.random.key(seed)
        k_x, k_w1, k_w2 = jax.random.split(key, 3)
        x = jax.random.normal(k_x, (4, 512, D_MODEL), dtype=jnp.float32)
        w1 = jax.random.normal(k_w1, (D_FF, D_MODEL), dtype=jnp.float32)
        b1 = jnp.zeros((D_FF,), dtype=jnp.float32)
        w2 = jax.random.normal(k_w2, (D_MODEL, D_FF), dtype=jnp.float32)
        b2 = jnp.zeros((D_MODEL,), dtype=jnp.float32)
        return {'x': x, 'w1': w1, 'b1': b1, 'w2': w2, 'b2': b2}
    _L0_ffn_in = _L0_ffn_setup()
    _d = {'L0_attn_hidden_states': _L0_attn_in['hidden_states'], 'L0_attn_Wq': _L0_attn_in['Wq'], 'L0_attn_Wk': _L0_attn_in['Wk'], 'L0_attn_Wv': _L0_attn_in['Wv'], 'L0_attn_Wo': _L0_attn_in['Wo'], 'L0_ffn_w1': _L0_ffn_in['w1'], 'L0_ffn_b1': _L0_ffn_in['b1'], 'L0_ffn_w2': _L0_ffn_in['w2'], 'L0_ffn_b2': _L0_ffn_in['b2']}
    _x0 = _d['L0_attn_hidden_states']
    _d['L0_attn_hidden_states'] = jax.random.normal(jax.random.fold_in(jax.random.key(seed), 1), (4, 1024, 256), dtype=_x0.dtype)
    del _x0
    return _d

def reference(L0_attn_hidden_states, L0_attn_Wq, L0_attn_Wk, L0_attn_Wv, L0_attn_Wo, L0_ffn_w1, L0_ffn_b1, L0_ffn_w2, L0_ffn_b2):

    def _L0_attn_ref(hidden_states, Wq, Wk, Wv, Wo):
        import jax, jax.numpy as jnp
        import numpy as np
        HID = 256
        H = 16
        KVH = 8
        D = HID // H
        WIN = 128
        KEEP = 0.33
        HOPS = 2
        ALPHA = 0.7
        NEG = -10000.0

        def _build_tls_mask(x):
            B, S, _ = x.shape
            norm = jnp.linalg.norm(x, axis=-1)
            mean = jnp.mean(x, axis=1, keepdims=True)
            mnorm = jnp.linalg.norm(mean, axis=-1)
            div = -jnp.sum(x * mean, axis=-1) / (norm * mnorm + 1e-06)
            score = ALPHA * norm + (1.0 - ALPHA) * div
            k = max(1, int(KEEP * S))
            _, idx = jax.lax.top_k(score, k)
            lm = jnp.zeros((B, S), bool).at[jnp.arange(B)[:, None], idx].set(True)
            for _ in range(HOPS):
                lm = lm | jnp.pad(lm[:, :-1], ((0, 0), (1, 0))) | jnp.pad(lm[:, 1:], ((0, 0), (0, 1)))
            i = jnp.arange(S)[:, None]
            j = jnp.arange(S)[None, :]
            causal = j <= i
            local = i - j < WIN
            mask = causal & (local | lm[:, None, :])
            return mask[:, None]
        B, S, _ = hidden_states.shape
        q = (hidden_states @ Wq).reshape(B, S, H, D).transpose(0, 2, 1, 3)
        k = (hidden_states @ Wk).reshape(B, S, KVH, D).transpose(0, 2, 1, 3)
        v = (hidden_states @ Wv).reshape(B, S, KVH, D).transpose(0, 2, 1, 3)
        k = jnp.repeat(k, H // KVH, axis=1)
        v = jnp.repeat(v, H // KVH, axis=1)
        mask = _build_tls_mask(hidden_states)
        scale = 1.0 / np.sqrt(D).astype(np.float32)
        scores = jnp.einsum('bhqd,bhkd->bhqk', q, k) * scale
        scores = scores + jnp.where(mask, jnp.float32(0.0), jnp.float32(NEG))
        probs = jax.nn.softmax(scores.astype(jnp.float32), axis=-1).astype(q.dtype)
        out = jnp.einsum('bhqk,bhkd->bhqd', probs, v)
        out = out.transpose(0, 2, 1, 3).reshape(B, S, HID)
        return out @ Wo

    def _L0_ffn_ref(x, w1, b1, w2, b2):
        import jax, jax.numpy as jnp
        import numpy as np
        D_MODEL = 256
        D_FF = 1024

        def absmean_quant(w):
            scale = jnp.mean(jnp.abs(w))
            mask = (jnp.abs(w) >= scale * 0.7).astype(w.dtype)
            return jnp.sign(w) * mask
        w1_q = absmean_quant(w1)
        w2_q = absmean_quant(w2)
        h = jnp.einsum('bsd,fd->bsf', x, w1_q) + b1
        h = jax.nn.gelu(h, approximate=False)
        out = jnp.einsum('bsf,df->bsd', h, w2_q) + b2
        return out
    x = L0_attn_hidden_states
    xn = _layernorm(x, axis=-1)
    s = _L0_attn_ref(xn, L0_attn_Wq, L0_attn_Wk, L0_attn_Wv, L0_attn_Wo)
    g = _silu(_L0_ffn_ref(xn, L0_ffn_w1, L0_ffn_b1, L0_ffn_w2, L0_ffn_b2))
    x = x + s * g
    return x

_drawn_inputs = setup_inputs


def setup_inputs(seed=0):
    import zlib

    import numpy as np

    out = dict(_drawn_inputs(seed))
    spreads = {'L0_ffn_b1': (0.0, 0.8), 'L0_ffn_b2': (0.0, 0.8)}
    factors = {}
    for name, (base, spread) in spreads.items():
        noise = np.random.default_rng([zlib.crc32(name.encode()), seed]).standard_normal(out[name].shape)
        drawn = base * np.exp(spread * noise) if base else spread * noise
        out[name] = jnp.asarray(drawn.astype(out[name].dtype))
    for name, factor in factors.items():
        out[name] = (out[name] * factor).astype(out[name].dtype)
    return out
```

```python
from contextlib import ExitStack

import concourse.bass as bass
from concourse import mybir

F32 = mybir.dt.float32
F32R = mybir.dt.float32r
BF16 = mybir.dt.bfloat16
I32 = mybir.dt.int32
ALU = mybir.AluOpType
ACT = mybir.ActivationFunctionType
AX_X = mybir.AxisListType.X
RMAX = bass.bass_isa.ReduceOp.max

P = 128
WIN = 128
KEEP, ALPHA, HOPS = 0.33, 0.7, 2
NEG = 10000.0
LN_EPS, DIV_EPS = 1e-5, 1e-6
EXP_MAX = 88.0
BOUND_MAX = 32.0
CH = 512
TC = CH // P


def kernel_program(nc, x, Wq, Wk, Wv, Wo, w1, b1, w2, b2, out):
    B, S, D = x.shape
    F = w1.shape[0]
    T = S // P
    NC = S // CH
    KD = D // P
    FT = F // P
    H, HD = 16, D // 16
    KVH = Wk.shape[1] // HD
    REP = H // KVH
    QT = H * HD // P
    HT = P // HD
    NQ = 4
    NPART = 6
    QPART = [0, 1, 2, 0, 1, 0]
    KPART = [0, 0, 0, 1, 1, 2]
    KROWS = NPART * HD
    SHIFT_ROWS = 3
    KEEPN = max(1, int(KEEP * S))
    VW = HD + 1
    assert (KD, QT, NC, T, KVH * HD) == (2, 2, 2, 8, P)

    STEPS = [(c, g, kb) for c in range(NC) for g in range(H // NQ) for kb in range(TC * (c + 1))]
    NSTEP = len(STEPS)
    NG = NC * H // NQ
    GROUP_END = [max(i for i, (c, g, _) in enumerate(STEPS) if c * (H // NQ) + g == n) for n in range(NG)]
    C1 = GROUP_END[H // NQ - 1] + 1
    LAG = 2

    def has_tri(i):
        return STEPS[i][2] >= TC * STEPS[i][0]

    def has_local(i):
        c, _, kb = STEPS[i]
        return TC * c <= kb + 1 < TC * (c + 1)

    def spans(i):
        c, _, kb = STEPS[i]
        lo = P * max(0, kb - TC * c)
        return lo, min(CH, max(lo, P * (kb + 2 - TC * c)))

    with ExitStack() as ctx:
        def sb(name, shape, dt=F32):
            return ctx.enter_context(nc.sbuf_tensor(name, shape, dt))

        def sem(name):
            s = ctx.enter_context(nc.semaphore(name))
            sems.append(s)
            return s

        sems = []
        ident = sb("ident", [P, P])
        ones = sb("ones", [P, P])
        before = sb("before", [P, P], BF16)
        after = sb("after", [P, P], BF16)
        band = sb("band", [P, 3, P], BF16)
        w1T = sb("w1T", [P, KD, F], F32R)
        w2T = sb("w2T", [P, FT, D], F32R)
        NW = 2 * D
        wqkv_hi = sb("wqkv_hi", [P, KD, NW], F32R)
        wqkv_lo = sb("wqkv_lo", [P, KD, NW], F32R)
        wo_sb = sb("wo_sb", [P, KD, D])
        b1_sb = sb("b1_sb", [P, FT])
        b2_bc = sb("b2_bc", [P, D])
        wsum = sb("wsum", [P, 2, T + 1])
        thr = sb("thr", [P, 2, 2])
        bound = sb("bound", [P, 8])
        shift = sb("shift", [P, 1])
        exact_flag = sb("exact_flag", [P, 1], I32)
        xn = sb("xn", [P, T, D])
        xT_hi = sb("xT_hi", [P, KD, S], F32R)
        xT_lo = sb("xT_lo", [P, KD, S], F32R)
        q_parts = sb("q_parts", [P, QT, 3, S], BF16)
        k_parts = sb("k_parts", [P, 3, S], BF16)
        q_stack = sb("q_stack", [P, H, S], BF16)
        k_stack = sb("k_stack", [P, KVH, S], BF16)
        v_sb = sb("v_sb", [P, T, KVH * VW + 32 - VW])
        probs = sb("probs", [P, 3, NQ, CH])
        local_mask = sb("local_mask", [P, T, P], BF16)
        key_bias = sb("key_bias", [P, T])
        landmark = sb("landmark", [P, T])
        hid = sb("hid", [P, 2, CH])
        h_hi = sb("h_hi", [P, FT, CH], F32R)
        h_lo = sb("h_lo", [P, FT, CH], F32R)
        zbuf = sb("zbuf", [P, D])
        ebuf = sb("ebuf", [P, D])
        gate = sb("gate", [P, TC, D])
        prod = sb("prod", [P, D])
        att_raw = sb("att_raw", [P, CH])
        attT = sb("attT", [P, QT, CH])
        den = sb("den", [P, P])
        rden = den
        rden_bc = sb("rden_bc", [P, QT, CH])
        resid = sb("resid", [P, CH])
        stats = sb("stats", [P, T, 6])
        mv = sb("mv", [P, T, 2])
        root_in = sb("root_in", [P, T + 1])
        root = sb("root", [P, T + 1])
        root_t = sb("root_t", [P, T + 1])
        rstd = sb("rstd", [P, T])
        ssq = sb("ssq", [P, T + 1])
        norm = sb("norm", [P, T + 1])
        colsum = sb("colsum", [P, KD, NC])
        mean = sb("mean", [P, KD])
        mean_sq = sb("mean_sq", [P, KD])
        mean_hl = sb("mean_hl", [P, KD, 2], F32R)
        dots = sb("dots", [P, 2 * T + 2])
        score = sb("score", [P, T])
        score_t = sb("score_t", [P, T])
        count = sb("count", [P, T, 4])
        lm_pad = sb("lm_pad", [P, T + 2], BF16)
        score_row = rden_bc[:, :, :].rearrange("p a n -> p (a n)")
        junk = resid[:, :].bitcast(BF16)
        w1_nat = probs[:, 0].rearrange("p a n -> p (a n)").rearrange("p (t d) -> p t d", d=D)
        w2_nat = probs[:, 1].rearrange("p a n -> p (a n)").rearrange("p (t f) -> p t f", f=F)
        head_block = hid[:, 0, 0:P]
        w_tmp = probs[:, 2].rearrange("p a n -> p (a n)")
        scratch = q_parts[:, :, :, :].rearrange("p a b n -> p (a b n)").bitcast(F32)
        w_nat = scratch[:, 0:KD * NW].rearrange("p (k n) -> p k n", k=KD)
        wk_rep = scratch[:, KD * NW:KD * NW + KD * D].rearrange("p (k n) -> p k n", k=KD)
        gram = scratch[:, KD * (NW + D):KD * (NW + D) + D]

        sc_ps = ctx.enter_context(nc.psum_tensor("sc_ps", [P, 4, CH], F32))
        att_ps = ctx.enter_context(nc.psum_tensor("att_ps", [P, 2, CH], F32))
        aux_ps = ctx.enter_context(nc.psum_tensor("aux_ps", [P, 2, CH], F32))

        dve_chain, act_chain, pool_chain = sem("dve_chain"), sem("act_chain"), sem("pool_chain")
        w1_in, w2_in, wqkv_in, wo_in, b_in, x_in = (sem(n) for n in ("w1_in", "w2_in", "wqkv_in", "wo_in", "b_in", "x_in"))
        consts_done, wabs_done, wtotal_done, tern_done, wT_done = (
            sem(n) for n in ("consts_done", "wabs_done", "wtotal_done", "tern_done", "wT_done"))
        wnat_split, gram_done, gram_sum_done, bound_sum_done, bound_ps_done, bound_max_done, bound_root_done = (
            sem(n) for n in ("wnat_split", "gram_done", "gram_sum_done", "bound_sum_done", "bound_ps_done",
                             "bound_max_done", "bound_root_done"))
        aux_done = sem("aux_done")
        aux_free = [sem("aux_free0"), sem("aux_free1")]
        aux_first = sem("aux_first")
        var_done, std_root, xn_done, xT_done = (sem(n) for n in ("var_done", "std_root", "xn_done", "xT_done"))
        mean_done, norm_in, norm_root, score_done, row_done, lm_done = (
            sem(n) for n in ("mean_done", "norm_in", "norm_root", "score_done", "row_done", "lm_done"))
        stack_in = [sem("stack_in0"), sem("stack_in1")]
        commit_done = sem("commit_done")
        sc_done, exp_done, tri_done, local_done, pv_done = (
            sem(n) for n in ("sc_done", "exp_done", "tri_done", "local_done", "pv_done"))
        att_out, att_in, rden_done, rden_in, attT_done = (
            sem(n) for n in ("att_out", "att_in", "rden_done", "rden_in", "attT_done"))
        hid_split, z_done, ez_done, prod_done, y_done, xres_in, y_out = (
            sem(n) for n in ("hid_split", "z_done", "ez_done", "prod_done", "y_done", "xres_in", "y_out"))

        def link(eng, chain, counter):
            def f(ins):
                counter[0] += 1
                ins.then_inc(chain, 1)
                eng.wait_ge(chain, counter[0])
            return f

        def clear_semaphores():
            with nc.Block(no_gpsimd_drain=True) as block:
                @block.sync
                def _(sp):
                    lo = min(s.num for s in sems)
                    assert [s.num for s in sems] == list(range(lo, lo + len(sems)))
                    sp.sem_clear(range(lo, lo + len(sems)))

        with nc.Block(no_gpsimd_drain=True) as block:
            @block.sync
            def _(sp):
                sp.dma_start(w1_nat, w1.rearrange("(t p) d -> p t d", p=P)).then_inc(w1_in, 16)
                sp.dma_start(w2_nat, w2.rearrange("(t p) f -> p t f", p=P)).then_inc(w2_in, 16)
                sp.dma_start(b1_sb[:, :], b1.rearrange("(t p) -> p t", p=P), allow_slow_non_contiguous=True).then_inc(b_in, 16)
                sp.dma_start(b2_bc[0:1, :], b2.rearrange("(a n) -> a n", a=1)).then_inc(b_in, 16)
                sp.wait_ge(b_in, 32)
                sp.wait_ge(x_in, 16)

            @block.scalar
            def _(act):
                act.dma_start(w_nat[:, :, 0:D], Wq.rearrange("(k p) n -> p k n", p=P)).then_inc(wqkv_in, 16)
                act.dma_start(w_nat[:, :, D:D + P], Wk.rearrange("(k p) n -> p k n", p=P)).then_inc(wqkv_in, 16)
                act.dma_start(w_nat[:, :, D + P:NW], Wv.rearrange("(k p) n -> p k n", p=P)).then_inc(wqkv_in, 16)
                act.dma_start(wo_sb[:, :, :], Wo.rearrange("(k p) n -> p k n", p=P)).then_inc(wo_in, 16)
                act.dma_start(xn[:, :, :], x[0].rearrange("(t p) d -> p t d", p=P)).then_inc(x_in, 16)
                for n in range(2 * KD * FT // TC):
                    act.wait_ge(wT_done, n + 1)
                    bank = [sc_ps, att_ps, aux_ps][min(n // 2, 2) if n >= 4 else 0]
                    src = sc_ps[:, n, :] if n < 4 else (att_ps[:, n - 4, :] if n < 6 else aux_ps[:, n - 6, :])
                    if n < 4:
                        dst = w1T[:, n // 2, (n % 2) * CH:(n % 2 + 1) * CH]
                    else:
                        dst = w2T[:, 2 * (n - 4):2 * (n - 3), :].rearrange("p t d -> p (t d)")
                    last = act.activation(dst, src, ACT.Copy)
                last.then_inc(tern_done, 1)
                act.wait_ge(bound_max_done, 2)
                act.activation(bound[:, 5:6], bound[:, 4:5], ACT.Sqrt).then_inc(bound_root_done, 1)
                act.wait_ge(wo_in, 16)

            @block.gpsimd
            def _(pool):
                lk = link(pool, pool_chain, [0])
                for t, v in ((ident, 0.0), (ones, 1.0), (before, 1.0), (after, 1.0), (hid, 1.0),
                             (band, 1.0), (v_sb, 0.0), (lm_pad, 0.0), (count, 0.0), (den, 1.0)):
                    last = pool.memset(t[tuple(slice(None) for _ in t.shape)], v)
                lk(last)

                def select(m, pattern, op, base, mult, fill):
                    lk(pool.affine_select(out=m, in_=m, compare_op=op, fill=fill, base=base,
                                          pattern=pattern, channel_multiplier=mult))
                select(ident[:, :], [[-1, P]], ALU.not_equal, 0, 1, 1.0)
                select(before[:, :], [[-1, P]], ALU.is_gt, 0, 1, 0.0)
                select(after[:, :], [[1, P]], ALU.is_gt, 0, -1, 0.0)
                hb = head_block.rearrange("p (g d) -> p g d", d=HD)
                select(hb, [[-HD, HT], [0, HD]], ALU.is_ge, 0, 1, 0.0)
                select(hb, [[HD, HT], [0, HD]], ALU.is_ge, HD - 1, -1, 0.0)
                select(band[:, 0, :], [[-1, P]], ALU.is_ge, HOPS - P, 1, 0.0)
                select(band[:, 1, :], [[-1, P]], ALU.is_ge, HOPS, 1, 0.0)
                select(band[:, 1, :], [[1, P]], ALU.is_ge, HOPS, -1, 0.0)
                select(band[:, 2, :], [[1, P]], ALU.is_ge, HOPS - P, -1, 0.0)
                pool.wait_ge(b_in, 32)
                pool.partition_broadcast(b2_bc[:, :], b2_bc[0:1, :]).then_inc(consts_done, 1)
                pool.wait_ge(bound_sum_done, 1)
                lk(pool.partition_all_reduce(bound[:, 2:4], bound[:, 0:2], P, RMAX))
                pool.sem_inc(bound_max_done, 1)
                lk(pool.memset(v_sb[:, :, 0:KVH * VW].rearrange("p t (j w) -> p t j w", w=VW)[:, :, :, HD:VW], 1.0))
                lk(pool.memset(q_stack[KROWS:KROWS + 32, :, :], 0.0))
                lk(pool.memset(k_stack[KROWS:KROWS + 32, :, :], 1.0))

            @block.vector
            def _(dve):
                lk = link(dve, dve_chain, [0])
                for n, (nat, s) in enumerate(((w1_nat, w1_in), (w2_nat, w2_in))):
                    dve.wait_ge(s, 16)
                    v = nat if n == 0 else nat.rearrange("p t f -> p (t f)").rearrange("p (t d) -> p t d", d=D)
                    lk(dve.tensor_reduce(wsum[:, n, 0:T], v, AX_X, ALU.add, apply_absolute_value=True))
                    dve.tensor_reduce(wsum[:, n, T:T + 1], wsum[:, n, 0:T], AX_X, ALU.add).then_inc(wabs_done, 1)
                dve.wait_ge(wqkv_in, 48)
                for lo in range(0, NW, P):
                    for k in range(KD):
                        src = w_nat[:, k, lo:lo + P]
                        hi, low = wqkv_hi[:, k, lo:lo + P], wqkv_lo[:, k, lo:lo + P]
                        if lo < D + P:
                            src = src.rearrange("p (h d) -> p h d", d=HD)
                            hi, low = (v.rearrange("p (d h) -> p h d", d=HD) for v in (hi, low))
                        lk(dve.tensor_copy(hi, src))
                        lk(dve.tensor_tensor(low, src, hi.bitcast(F32), ALU.subtract))
                for k in range(KD):
                    for r in range(REP):
                        last = dve.tensor_copy(wk_rep[:, k, :].rearrange("p (j r d) -> p j r d", j=KVH, r=REP)[:, :, r, :],
                                               w_nat[:, k, D:D + P].rearrange("p (j d) -> p j d", j=KVH))
                last.then_inc(wnat_split, 1)
                dve.wait_ge(wtotal_done, 1)
                lk(dve.tensor_scalar(thr[:, :, 0], aux_ps[:, 0, 0:2], 1.0 / (F * D), 0.7, ALU.mult, ALU.mult))
                lk(dve.tensor_scalar(thr[:, :, 1], thr[:, :, 0], -1.0, None, ALU.mult))
                for n, nat in enumerate((w1_nat, w2_nat)):
                    flat = nat.rearrange("p a n -> p (a n)")
                    lk(dve.tensor_scalar(w_tmp, flat, thr[:, n, 1:2], None, ALU.is_le))
                    ins = dve.scalar_tensor_tensor(flat, flat, thr[:, n, 0:1], w_tmp, ALU.is_ge, ALU.subtract)
                    ins.then_inc(wabs_done, 1)
                    dve.wait_ge(wabs_done, 3 + n)
                dve.wait_ge(gram_done, 1)
                lk(dve.tensor_copy(gram, aux_ps[:, 1, 0:D]))
                lk(dve.tensor_tensor(gram, gram, aux_ps[:, 1, D:2 * D], ALU.mult))
                for m in range(QT):
                    lk(dve.tensor_tensor(gram[:, m * P:(m + 1) * P], gram[:, m * P:(m + 1) * P], head_block, ALU.mult))
                dve.tensor_reduce(bound[:, 6:8], gram.rearrange("p (m n) -> p m n", n=P), AX_X, ALU.add).then_inc(gram_sum_done, 1)
                dve.wait_ge(bound_ps_done, 1)
                dve.tensor_copy(bound[:, 0:2], aux_ps[:, 0, 8:10]).then_inc(bound_sum_done, 1)
                dve.wait_ge(bound_max_done, 1)
                dve.tensor_reduce(bound[:, 4:5], bound[:, 2:4], AX_X, ALU.max).then_inc(bound_max_done, 1)
                dve.wait_ge(bound_root_done, 1)
                lk(dve.tensor_scalar(bound[:, 6:7], bound[:, 5:6], 1.001 * D / HD ** 0.5, None, ALU.mult))
                lk(dve.tensor_scalar(bound[:, 7:8], bound[:, 6:7], BOUND_MAX, None, ALU.is_le))
                lk(dve.tensor_scalar(exact_flag[:, :], bound[:, 7:8], -1.0, 1.0, ALU.mult, ALU.add))
                lk(dve.tensor_scalar(bound[:, 6:7], bound[:, 6:7], BOUND_MAX, -1.0, ALU.min, ALU.mult))
                lk(dve.tensor_tensor(shift[:, :], bound[:, 6:7], bound[:, 7:8], ALU.mult))

            @block.tensor
            def _(pe):
                pe.wait_ge(consts_done, 1)
                pe.wait_ge(wabs_done, 2)
                pe.matmul(aux_ps[:, 0, 0:2], ones[:, :], wsum[:, :, T], start=True, stop=True).then_inc(wtotal_done, 1)
                pe.wait_ge(wnat_split, 1)
                for n, w in enumerate((w_nat, wk_rep)):
                    for m in range(QT):
                        for k in range(KD):
                            last = pe.matmul(aux_ps[:, 1, (QT * n + m) * P:(QT * n + m + 1) * P], w[:, k, m * P:(m + 1) * P],
                                             w[:, k, m * P:(m + 1) * P], start=(k == 0), stop=(k == KD - 1))
                last.then_inc(gram_done, 1)
                for n in range(2 * KD * FT // TC):
                    if n in (0, 4):
                        pe.wait_ge(wabs_done, 3 + n // 4)
                    if n == 6:
                        pe.wait_ge(gram_sum_done, 1)
                        pe.matmul(aux_ps[:, 0, 8:10], head_block, bound[:, 6:8], start=True, stop=True).then_inc(bound_ps_done, 1)
                        pe.wait_ge(bound_sum_done, 1)
                    dst = sc_ps[:, n, :] if n < 4 else (att_ps[:, n - 4, :] if n < 6 else aux_ps[:, n - 6, :])
                    for q in range(TC):
                        if n < 4:
                            src = w1_nat[:, (n % 2) * TC + q, (n // 2) * P:(n // 2 + 1) * P]
                        else:
                            f = 2 * (n - 4) + q // 2
                            src = w2_nat[:, q % 2, f * P:(f + 1) * P]
                        last = pe.transpose(dst[:, q * P:(q + 1) * P], src, ident[:, :])
                    last.then_inc(wT_done, 1)
        clear_semaphores()

        def jobs_of(main, prep):
            jobs = []
            if main:
                jobs += [(-1, "ffn_up", 0, f) for f in range(FT)]
                jobs += [(3 * (t + 1), "ffn_down", t) for t in range(TC)]
                jobs += [(C1 - 0.5, "ffn_up", 1, f) for f in range(FT)]
                jobs += [(C1 + 11 + 2 * t, "ffn_down", TC + t) for t in range(TC)]
                jobs += [(C1 + 10 + 2 * t, "out_proj", t) for t in range(TC)]
                jobs += [(NSTEP + 5, "out_proj", TC + t) for t in range(TC)]
            if prep:
                s = C1 if main else 0
                jobs += [(s + 3 + 2 * c, "transpose", k, c) for c in range(NC) for k in range(KD)]
                jobs += [(s + 7 + c, "k_proj", c) for c in range(NC)]
                jobs += [(s + 9 + 2 * m + c, "q_proj", m, c) for m in range(QT) for c in range(NC)]
                jobs += [(s + 9.5, "mean_dot")]
                jobs += [(s + 15.5, "score_row", i) for i in range(2)]
                jobs += [(s + 27.5, "dilate")]
                jobs += [(NSTEP + 3, "v_proj", i) for i in range(2)]
            return sorted(jobs, key=lambda j: j[0])

        RANK_AT = 17

        def turn(b, main, prep, x_next):
            jobs = jobs_of(main, prep)
            S0 = C1 if main else 0
            last_step = NSTEP + 5

            def jobs_at(lo, hi):
                return [(n,) + j[1:] for n, j in enumerate(jobs) if lo <= j[0] < hi]

            n_transposes = [n for n, j in enumerate(jobs) if j[1] == "transpose"]

            with nc.Block(no_gpsimd_drain=True) as block:
                @block.sync
                def _(sp):
                    if main:
                        for c in range(NC):
                            cs = slice(c * CH, (c + 1) * CH)
                            for i in range(NPART):
                                rows = slice(i * HD, (i + 1) * HD)
                                sp.dma_start(k_stack[rows, :, cs], k_parts[:, KPART[i], cs]).then_inc(stack_in[c], 16)
                                for m in range(QT):
                                    sp.dma_start(q_stack[rows, m * HT:(m + 1) * HT, cs],
                                                 q_parts[:, m, QPART[i], cs]).then_inc(stack_in[c], 16)
                    if prep and main:
                        sp.dma_start(xn[:, :, :], x_next.rearrange("(t p) d -> p t d", p=P)).then_inc(x_in, 16)

                    def att_group(n):
                        c, g = n // (H // NQ), n % (H // NQ)
                        sp.wait_ge(att_out, n + 1)
                        if c == 1 and g == 0:
                            sp.wait_ge(aux_done, 1 + max(i for i, j in enumerate(jobs) if j[1] == "out_proj" and j[2] < TC))
                        h = g * NQ
                        for q in range(NQ):
                            row = (h % HT + q) * HD
                            sp.dma_start(attT[row:row + HD, h // HT, :], att_raw[32 * q:32 * q + HD, :]).then_inc(att_in, 16)
                        sp.dma_start(den[h * TC:(h + NQ) * TC, :], att_raw[HD:P:32, :]).then_inc(att_in, 16)

                    def spread_rden(c):
                        sp.wait_ge(rden_done, c + 1)
                        for m in range(QT):
                            for s in range(TC):
                                src = rden[m * HT * TC + s:(m + 1) * HT * TC:TC, :]
                                sp.dma_start(rden_bc[:, m, s * P:(s + 1) * P],
                                             src.unsqueeze(1).to_broadcast([HT, HD, P])).then_inc(rden_in, 16)

                    if main:
                        xb = x[b].rearrange("(t p) d -> p t d", p=P)
                        ob = out[b].rearrange("(t p) d -> p t d", p=P)
                        for n in range(4):
                            att_group(n)
                        spread_rden(0)
                        if prep:
                            sp.wait_ge(aux_done, n_transposes[-1] + 1)
                        sp.dma_start(xn[:, :, :], xb).then_inc(xres_in, 16)
                        for n in range(4, 6):
                            att_group(n)
                        sp.wait_ge(y_done, TC)
                        sp.dma_start(ob[:, 0:TC, :], xn[:, 0:TC, :]).then_inc(y_out, 16)
                        for n in range(6, 8):
                            att_group(n)
                        spread_rden(1)
                        sp.wait_ge(y_done, 2 * TC)
                        sp.dma_start(ob[:, TC:T, :], xn[:, TC:T, :]).then_inc(y_out, 16)
                        sp.wait_ge(y_out, 32)

                @block.tensor
                def _(pe):
                    def job(n, kind, *a):
                        ps = aux_ps[:, n % 2, :]
                        if n >= 2:
                            pe.wait_ge(aux_free[n % 2], n // 2)
                        if kind == "ffn_up":
                            c, f = a
                            for k in range(KD):
                                for part in (xT_hi, xT_lo):
                                    last = pe.matmul(ps, w1T[:, k, f * P:(f + 1) * P], part[:, k, c * CH:(c + 1) * CH],
                                                     start=(k == 0 and part is xT_hi), stop=(k == KD - 1 and part is xT_lo))
                        elif kind == "ffn_down":
                            t, = a
                            pe.wait_ge(hid_split, FT * (t // TC + 1))
                            q = t % TC
                            for f in range(FT):
                                for part in (h_hi, h_lo):
                                    last = pe.matmul(ps[:, 0:D], part[:, f, q * P:(q + 1) * P], w2T[:, f, :],
                                                     start=(f == 0 and part is h_hi), stop=(f == FT - 1 and part is h_lo))
                        elif kind == "out_proj":
                            t, = a
                            pe.wait_ge(attT_done, t // TC + 1)
                            q = t % TC
                            for k in range(KD):
                                last = pe.matmul(ps[:, 0:D], attT[:, k, q * P:(q + 1) * P], wo_sb[:, k, :],
                                                 start=(k == 0), stop=(k == KD - 1))
                        elif kind == "transpose":
                            k, c = a
                            pe.wait_ge(xn_done, TC * (c + 1))
                            for q in range(TC):
                                last = pe.transpose(ps[:, q * P:(q + 1) * P], xn[:, c * TC + q, k * P:(k + 1) * P], ident[:, :])
                        elif kind in ("k_proj", "q_proj"):
                            m, c = a if kind == "q_proj" else (QT, a[0])
                            pe.wait_ge(xT_done, KD * NC)
                            ws, xs = slice(m * P, (m + 1) * P), slice(c * CH, (c + 1) * CH)
                            mms = [(w, xp, k) for k in range(KD) for w, xp in ((wqkv_hi, xT_hi), (wqkv_hi, xT_lo), (wqkv_lo, xT_hi))]
                            for i, (w, xp, k) in enumerate(mms):
                                last = pe.matmul(ps, w[:, k, ws], xp[:, k, xs], start=(i == 0), stop=(i == len(mms) - 1))
                        elif kind == "v_proj":
                            for q in range(TC):
                                t = a[0] * TC + q
                                mms = [(xp, w, k) for k in range(KD) for xp, w in ((xT_hi, wqkv_hi), (xT_lo, wqkv_hi), (xT_hi, wqkv_lo))]
                                for i, (xp, w, k) in enumerate(mms):
                                    last = pe.matmul(ps[:, q * P:(q + 1) * P], xp[:, k, t * P:(t + 1) * P], w[:, k, D + P:NW],
                                                     start=(i == 0), stop=(i == len(mms) - 1))
                        elif kind == "mean_dot":
                            pe.wait_ge(mean_done, 1)
                            for t in range(T):
                                for k in range(KD):
                                    for part in (xT_hi, xT_lo):
                                        pe.matmul(ps[:, 2 * t:2 * t + 2], part[:, k, t * P:(t + 1) * P], mean_hl[:, k, :],
                                                  start=(k == 0 and part is xT_hi), stop=(k == KD - 1 and part is xT_lo))
                            for k in range(KD):
                                last = pe.matmul(ps[:, 2 * T:2 * T + 1], ones[:, :], mean_sq[:, k:k + 1],
                                                 start=(k == 0), stop=(k == KD - 1))
                        elif kind == "score_row":
                            pe.wait_ge(score_done, 1)
                            for q in range(TC):
                                t = a[0] * TC + q
                                last = pe.transpose(ps[:, q * P:(q + 1) * P], score[:, t:t + 1].to_broadcast([P, P]), ident[:, :])
                        elif kind == "dilate":
                            pe.wait_ge(lm_done, 1)
                            for i in range(3):
                                last = pe.matmul(ps[:, 0:T], band[:, i, :], lm_pad[:, i:i + T], start=(i == 0), stop=(i == 2))
                        last.then_inc(aux_done, 1)

                    def scores(i):
                        c, g, kb = STEPS[i]
                        if i in (0, C1):
                            pe.wait_ge(stack_in[c], 16 * NPART * (1 + QT))
                        lo = spans(i)[0]
                        for u in range(2):
                            if i >= 1:
                                pe.wait_ge(exp_done, 2 * (i - 1) + u + 1)
                            for hh in range(2):
                                h = g * NQ + 2 * u + hh
                                last = pe.matmul(sc_ps[:, 2 * u + hh, lo:CH], k_stack[0:KROWS + SHIFT_ROWS, h // REP, kb * P:(kb + 1) * P],
                                                 q_stack[0:KROWS + SHIFT_ROWS, h, c * CH + lo:(c + 1) * CH], start=True, stop=True)
                            last.then_inc(sc_done, 1)

                    def values(i):
                        c, g, kb = STEPS[i]
                        n = c * (H // NQ) + g
                        if kb == 0 and n >= 2:
                            pe.wait_ge(att_out, n - 1)
                        if i == 0:
                            pe.wait_ge(commit_done, 1)
                        pe.wait_ge(exp_done, 2 * (i + 1))
                        if has_tri(i):
                            pe.wait_ge(tri_done, sum(has_tri(j) for j in range(i + 1)))
                        if has_local(i):
                            pe.wait_ge(local_done, sum(has_local(j) for j in range(i + 1)))
                        lo = spans(i)[0]
                        for q in range(NQ):
                            j = (g * NQ + q) // REP
                            last = pe.matmul(att_ps[32 * q:32 * q + 32, n % 2, lo:CH], v_sb[:, kb, j * VW:j * VW + 32],
                                             probs[:, i % 3, q, lo:CH], start=(kb == 0), stop=(kb == TC * (c + 1) - 1))
                        last.then_inc(pv_done, 1)

                    for j in jobs_at(-9, 0):
                        job(*j)
                    if main:
                        for i in range(NSTEP + LAG):
                            for j in jobs_at(i - 0.5, i):
                                job(*j)
                            if i < NSTEP:
                                scores(i)
                            for j in jobs_at(i, i + 0.5):
                                job(*j)
                            if i >= LAG:
                                values(i - LAG)
                        for j in jobs_at(NSTEP + LAG - 0.5, 999):
                            job(*j)
                    else:
                        for j in jobs_at(0, 999):
                            job(*j)

                @block.scalar
                def _(act):
                    def job(n, kind, *a):
                        ps = aux_ps[:, n % 2, :]
                        if kind == "ffn_up":
                            c, f = a
                            u = c * FT + f
                            act.wait_ge(aux_done, n + 1)
                            if u >= 2:
                                act.wait_ge(hid_split, u - 1)
                            act.activation(hid[:, u % 2, :], ps, ACT.Gelu, bias=b1_sb[:, f:f + 1]).then_inc(aux_free[n % 2], 1)
                        elif kind == "transpose":
                            k, c = a
                            act.wait_ge(aux_done, n + 1)
                            act.activation(xT_hi[:, k, c * CH:(c + 1) * CH], ps, ACT.Copy).then_inc(aux_first, 1)
                        elif kind in ("k_proj", "q_proj"):
                            dst = k_parts[:, 0, a[0] * CH:(a[0] + 1) * CH] if kind == "k_proj" else \
                                q_parts[:, a[0], 0, a[1] * CH:(a[1] + 1) * CH]
                            act.wait_ge(aux_done, n + 1)
                            if main:
                                act.wait_ge(stack_in[1], 16 * NPART * (1 + QT))
                            act.activation(dst, ps, ACT.Copy).then_inc(aux_first, 1)
                        elif kind == "v_proj":
                            act.wait_ge(aux_done, n + 1)
                            for q in range(TC):
                                t = a[0] * TC + q
                                last = act.activation(v_sb[:, t, 0:KVH * VW].rearrange("p (j w) -> p j w", w=VW)[:, :, 0:HD],
                                                      ps[:, q * P:(q + 1) * P].rearrange("p (j d) -> p j d", d=HD), ACT.Copy)
                            last.then_inc(aux_free[n % 2], 1)
                        elif kind == "score_row":
                            act.wait_ge(aux_done, n + 1)
                            act.activation(score_row[:, a[0] * CH:(a[0] + 1) * CH], ps, ACT.Copy).then_inc(row_done, 1)
                            act.wait_ge(row_done, a[0] + 1)
                            act.sem_inc(aux_free[n % 2], 1)
                        elif kind == "ffn_down":
                            t, = a
                            act.wait_ge(z_done, t + 1)
                            act.activation(ebuf[:, :], ebuf[:, :], ACT.Exp, scale=-1.0).then_inc(ez_done, 1)

                    def roots(m, k, ready, done):
                        act.wait_ge(ready, 1)
                        act.activation(root[:, 0:m], root_in[:, 0:m], ACT.Sqrt).then_inc(done, 1)

                    def exps(i):
                        c, g, kb = STEPS[i]
                        lo, near = spans(i)
                        if i == 0:
                            act.wait_ge(commit_done, 1)
                        if i >= 3:
                            act.wait_ge(pv_done, i - 2)
                        for u in range(2):
                            act.wait_ge(sc_done, 2 * i + u + 1)
                            us = slice(2 * u, 2 * u + 2)
                            if near > lo:
                                last = act.activation(probs[:, i % 3, us, lo:near], sc_ps[:, us, lo:near], ACT.Exp,
                                                      bias=shift[:, 0:1], scale=HD ** -0.5)
                            if near < CH:
                                last = act.activation(probs[:, i % 3, us, near:CH], sc_ps[:, us, near:CH], ACT.Exp,
                                                      bias=key_bias[:, kb:kb + 1], scale=HD ** -0.5)
                            last.then_inc(exp_done, 1)

                    if prep and not main:
                        roots(T, 0, var_done, std_root)
                    for j in jobs_at(-9, 0):
                        job(*j)
                    for i in range(NSTEP if main else last_step + 1):
                        if prep and main and i == C1:
                            roots(T, 0, var_done, std_root)
                        for j in jobs_at(i - 0.5, i):
                            job(*j)
                        if prep and i == S0 + 12:
                            roots(T + 1, 1, norm_in, norm_root)
                        if main:
                            exps(i)
                        for j in jobs_at(i, i + 0.5):
                            job(*j)
                    if main:
                        for j in jobs_at(NSTEP - 0.5, 999):
                            job(*j)

                @block.gpsimd
                def _(pool):
                    def residual(t):
                        if t == 0:
                            pool.wait_ge(xres_in, 16)
                        pool.wait_ge(prod_done, t + 1)
                        pool.tensor_tensor(xn[:, t, :], xn[:, t, :], prod[:, :], ALU.add).then_inc(y_done, 1)

                    if main:
                        for i in range(NSTEP):
                            if has_tri(i):
                                c, g, kb = STEPS[i]
                                pool.wait_ge(exp_done, 2 * (i + 1))
                                tile = probs[:, i % 3, :, P * (kb - TC * c):P * (kb - TC * c + 1)]
                                pool.affine_select(out=tile, in_=tile, compare_op=ALU.is_ge, fill=0.0, base=0,
                                                   pattern=[[0, NQ], [1, P]], channel_multiplier=-1).then_inc(tri_done, 1)
                            for _, kind, *a in jobs_at(i - 0.5, i + 0.5):
                                if kind == "out_proj":
                                    residual(a[0])
                        for t in range(TC, T):
                            residual(t)

                @block.vector
                def _(dve):
                    lk = link(dve, dve_chain, [0])

                    def newton(m):
                        lk(dve.tensor_scalar(root_t[:, 0:m], root[:, 0:m], 1e-30, None, ALU.max))
                        lk(dve.reciprocal(root_t[:, 0:m], root_t[:, 0:m]))
                        lk(dve.tensor_tensor(root_t[:, 0:m], root_t[:, 0:m], root_in[:, 0:m], ALU.mult))
                        lk(dve.tensor_tensor(root_t[:, 0:m], root_t[:, 0:m], root[:, 0:m], ALU.add))
                        lk(dve.tensor_scalar(norm[:, 0:m], root_t[:, 0:m], 0.5, None, ALU.mult))

                    def commit():
                        lk(dve.tensor_scalar(key_bias[:, :], landmark[:, :], -1.0, NEG, ALU.add, ALU.mult))
                        lk(dve.tensor_scalar(key_bias[:, :], key_bias[:, :], shift[:, 0:1], None, ALU.add))
                        for t in range(T):
                            last = dve.tensor_scalar(local_mask[:, t, :], before[:, :], landmark[:, t:t + 1], None, ALU.max)
                        last.then_inc(commit_done, 1)

                    def local(i):
                        c, g, kb = STEPS[i]
                        lo = P * (kb + 1 - TC * c)
                        dve.wait_ge(exp_done, 2 * (i + 1))
                        tile = probs[:, i % 3, :, lo:lo + P]
                        for q in range(NQ):
                            last = dve.scalar_tensor_tensor(tile[:, q, :], tile[:, q, :], 3e38, local_mask[:, kb, :], ALU.min, ALU.mult)
                        last.then_inc(local_done, 1)

                    def job(n, kind, *a):
                        ps = aux_ps[:, n % 2, :]
                        if kind == "ffn_up":
                            c, f = a
                            u = c * FT + f
                            dve.wait_ge(aux_free[n % 2], n // 2 + 1)
                            lk(dve.tensor_copy(h_hi[:, f, :], hid[:, u % 2, :]))
                            dve.tensor_tensor(h_lo[:, f, :], hid[:, u % 2, :], h_hi[:, f, :].bitcast(F32), ALU.subtract).then_inc(hid_split, 1)
                        elif kind == "ffn_down":
                            t, = a
                            dve.wait_ge(aux_done, n + 1)
                            lk(dve.tensor_tensor(zbuf[:, :], ps[:, 0:D], b2_bc[:, :], ALU.add))
                            dve.sem_inc(aux_free[n % 2], 1)
                            dve.tensor_scalar(ebuf[:, :], zbuf[:, :], -EXP_MAX, None, ALU.max).then_inc(z_done, 1)
                        elif kind == "out_proj":
                            t, = a
                            dve.wait_ge(aux_done, n + 1)
                            if t >= 1:
                                dve.wait_ge(y_done, t)
                            dve.tensor_tensor(prod[:, :], ps[:, 0:D], gate[:, t % TC, :], ALU.mult).then_inc(prod_done, 1)
                            dve.wait_ge(prod_done, t + 1)
                            dve.sem_inc(aux_free[n % 2], 1)
                        elif kind == "transpose":
                            k, c = a
                            m = c * KD + k
                            dve.wait_ge(aux_first, m + 1)
                            dve.tensor_tensor(xT_lo[:, k, c * CH:(c + 1) * CH], ps,
                                              xT_hi[:, k, c * CH:(c + 1) * CH].bitcast(F32), ALU.subtract).then_inc(xT_done, 1)
                            dve.tensor_reduce(colsum[:, k, c:c + 1], ps, AX_X, ALU.add).then_inc(aux_free[n % 2], 1)
                            if m == KD * NC - 1:
                                dve.wait_ge(aux_free[n % 2], n // 2 + 1)
                                lk(dve.tensor_tensor(mean[:, :], colsum[:, :, 0], colsum[:, :, 1], ALU.add))
                                lk(dve.tensor_scalar(mean[:, :], mean[:, :], 1.0 / S, None, ALU.mult))
                                lk(dve.tensor_copy(mean_hl[:, :, 0], mean[:, :]))
                                lk(dve.tensor_tensor(mean_hl[:, :, 1], mean[:, :], mean_hl[:, :, 0].bitcast(F32), ALU.subtract))
                                dve.tensor_tensor(mean_sq[:, :], mean[:, :], mean[:, :], ALU.mult).then_inc(mean_done, 1)
                        elif kind in ("k_proj", "q_proj"):
                            first = KD * NC + (a[0] if kind == "k_proj" else NC + a[0] * NC + a[1])
                            c = a[0] if kind == "k_proj" else a[1]
                            part = [(k_parts[:, r, c * CH:(c + 1) * CH] if kind == "k_proj" else
                                     q_parts[:, a[0], r, c * CH:(c + 1) * CH]) for r in range(3)]
                            dve.wait_ge(aux_first, first + 1)
                            ins = dve.tensor_tensor(resid[:, :], ps, part[0], ALU.subtract)
                            ins.then_inc(aux_free[n % 2], 1)
                            dve.wait_ge(aux_free[n % 2], n // 2 + 1)
                            lk(dve.tensor_copy(part[1], resid[:, :]))
                            lk(dve.tensor_tensor(part[2], resid[:, :], part[1], ALU.subtract))
                        elif kind == "mean_dot":
                            dve.wait_ge(aux_done, n + 1)
                            dve.tensor_copy(dots[:, 0:2 * T + 1], ps[:, 0:2 * T + 1]).then_inc(aux_free[n % 2], 1)
                            dve.wait_ge(aux_free[n % 2], n // 2 + 1)
                            dve.tensor_copy(root_in[:, 0:T], ssq[:, 0:T])
                            dve.tensor_copy(root_in[:, T:T + 1], dots[:, 2 * T:2 * T + 1]).then_inc(norm_in, 1)
                        elif kind == "dilate":
                            dve.wait_ge(aux_done, n + 1)
                            dve.tensor_scalar(landmark[:, :], ps[:, 0:T], 1.0, None, ALU.min).then_inc(aux_free[n % 2], 1)

                    def silu(t):
                        dve.wait_ge(ez_done, t + 1)
                        e = ebuf[:, :]
                        lk(dve.tensor_scalar(e, e, 1.0, None, ALU.add))
                        lk(dve.reciprocal(e, e))
                        lk(dve.tensor_tensor(gate[:, t % TC, :], zbuf[:, :], e, ALU.mult))

                    def layer_norm(k):
                        if k < T:
                            if k == 0 and main:
                                dve.wait_ge(x_in, 16)
                            lk(dve.bn_stats(stats[:, k, :], xn[:, k, :]))
                            lk(dve.bn_aggr(mv[:, k, :], stats[:, k, :]))
                        elif k == T:
                            dve.tensor_scalar(root_in[:, 0:T], mv[:, :, 1], LN_EPS, None, ALU.add).then_inc(var_done, 1)

                    def normalise_x(t):
                        if t == 0:
                            dve.wait_ge(std_root, 1)
                            newton(T)
                            lk(dve.reciprocal(rstd[:, :], norm[:, 0:T]))
                        dve.tensor_scalar(xn[:, t, :], xn[:, t, :], mv[:, t, 0:1], rstd[:, t:t + 1], ALU.subtract, ALU.mult).then_inc(xn_done, 1)
                        dve.wait_ge(xn_done, t + 1)
                        lk(dve.scalar_tensor_tensor(resid[:, 0:D], xn[:, t, :], 1.0, xn[:, t, :], ALU.mult, ALU.mult,
                                                    accum_out=ssq[:, t:t + 1]))

                    def token_scores():
                        dve.wait_ge(norm_root, 1)
                        newton(T + 1)
                        lk(dve.tensor_tensor(score_t[:, :], dots[:, 0:2 * T:2], dots[:, 1:2 * T:2], ALU.add))
                        lk(dve.tensor_scalar(root_t[:, 0:T], norm[:, 0:T], norm[:, T:T + 1], DIV_EPS, ALU.mult, ALU.add))
                        lk(dve.reciprocal(root_t[:, 0:T], root_t[:, 0:T]))
                        lk(dve.tensor_tensor(score_t[:, :], score_t[:, :], root_t[:, 0:T], ALU.mult))
                        lk(dve.tensor_scalar(score_t[:, :], score_t[:, :], -(1.0 - ALPHA), None, ALU.mult))
                        lk(dve.tensor_scalar(score[:, :], norm[:, 0:T], ALPHA, None, ALU.mult))
                        dve.tensor_tensor(score[:, :], score[:, :], score_t[:, :], ALU.add).then_inc(score_done, 1)

                    def rank(t):
                        if t == 0:
                            dve.wait_ge(score_done, 1)
                            dve.wait_ge(row_done, 2)
                        own, at = score[:, t:t + 1], slice(t * P, (t + 1) * P)
                        if t > 0:
                            lk(dve.tensor_scalar(junk[:, 0:t * P], score_row[:, 0:t * P], own, 0.0, ALU.is_ge, ALU.add,
                                                 accum_out=count[:, t, 0:1]))
                        if t < T - 1:
                            lk(dve.tensor_scalar(junk[:, 0:S - (t + 1) * P], score_row[:, (t + 1) * P:S], own, 0.0, ALU.is_gt, ALU.add,
                                                 accum_out=count[:, t, 1:2]))
                        lk(dve.scalar_tensor_tensor(junk[:, 0:P], score_row[:, at], own, before[:, :], ALU.is_ge, ALU.mult,
                                                    accum_out=count[:, t, 2:3]))
                        lk(dve.scalar_tensor_tensor(junk[:, 0:P], score_row[:, at], own, after[:, :], ALU.is_gt, ALU.mult,
                                                    accum_out=count[:, t, 3:4]))
                        if t == T - 1:
                            lk(dve.tensor_reduce(score_t[:, :], count[:, :, :], AX_X, ALU.add))
                            dve.tensor_scalar(lm_pad[:, 1:T + 1], score_t[:, :], float(KEEPN), None, ALU.is_lt).then_inc(lm_done, 1)

                    def group_out(n):
                        dve.wait_ge(pv_done, GROUP_END[n] + 1)
                        if n >= 1:
                            dve.wait_ge(att_in, 16 * (NQ + 1) * n)
                        dve.tensor_copy(att_raw[:, :], att_ps[:, n % 2, :]).then_inc(att_out, 1)

                    def reciprocals(c):
                        dve.wait_ge(att_in, 16 * (NQ + 1) * (H // NQ) * (c + 1))
                        dve.reciprocal(rden[0:H * TC, :], den[0:H * TC, :]).then_inc(rden_done, 1)

                    def normalise_heads(c):
                        dve.wait_ge(rden_in, 16 * QT * TC * (c + 1))
                        dve.tensor_tensor(attT[:, :, :], attT[:, :, :], rden_bc[:, :, :], ALU.mult).then_inc(attT_done, 1)

                    if main:
                        commit()
                    if prep and not main:
                        for k in range(T + 1):
                            layer_norm(k)
                    for j in jobs_at(-9, 0):
                        job(*j)
                    for i in range(last_step + 1 if not main else NSTEP + LAG):
                        for j in jobs_at(i - 0.5, i):
                            job(*j)
                        if main and i < NSTEP and has_local(i):
                            local(i)
                        for j in jobs_at(i, i + 0.5):
                            job(*j)
                        if main:
                            for n in range(NG):
                                if GROUP_END[n] + LAG == i:
                                    group_out(n)
                            for _, kind, *a in jobs_at(i - 1.5, i - 0.5):
                                if kind == "ffn_down":
                                    silu(a[0])
                            if i == C1 + 5:
                                reciprocals(0)
                            if i == C1 + 8:
                                normalise_heads(0)
                            if prep and 1 <= i < T + 2:
                                layer_norm(i - 1)
                        if prep:
                            if S0 <= i < S0 + T // 2:
                                normalise_x(2 * (i - S0))
                                normalise_x(2 * (i - S0) + 1)
                            if i == S0 + 13:
                                token_scores()
                            if S0 + RANK_AT <= i < S0 + RANK_AT + T:
                                rank(i - S0 - RANK_AT)
                    if main:
                        reciprocals(1)
                        normalise_heads(1)
                        for j in jobs_at(NSTEP + LAG - 0.5, 999):
                            job(*j)
            clear_semaphores()

        turn(None, False, True, None)
        with nc.Fori(0, B - 1) as b:
            turn(b, True, True, x[b + 1])
        turn(B - 1, True, False, None)


_INS = ["L0_attn_hidden_states", "L0_attn_Wq", "L0_attn_Wk", "L0_attn_Wv", "L0_attn_Wo",
        "L0_ffn_w1", "L0_ffn_b1", "L0_ffn_w2", "L0_ffn_b2"]


def kernel(**inputs):
    import numpy as _np
    import concourse.bacc as _bacc
    from concourse import mybir as _mybir
    from concourse.bass_utils import run_bass_kernel_spmd as _run

    nc = _bacc.Bacc("TRN2", target_bir_lowering=False, num_devices=1)
    arrays, args = {}, []
    for name in _INS:
        a = _np.ascontiguousarray(inputs[name])
        arrays[f"in_{name}"] = a
        args.append(nc.dram_tensor(f"in_{name}", a.shape, _mybir.dt.from_np(a.dtype), kind="ExternalInput").ap())
    shape = inputs["L0_attn_hidden_states"].shape
    args.append(nc.dram_tensor("out_y", shape, _mybir.dt.float32, kind="ExternalOutput").ap())
    kernel_program(nc, *args)
    r = _run(nc, [arrays], core_ids=[0])
    return r.results[0]["out_y"]
```

```python
from contextlib import ExitStack

import concourse.bass as bass
from concourse import mybir

F32 = mybir.dt.float32
F32R = mybir.dt.float32r
BF16 = mybir.dt.bfloat16
I32 = mybir.dt.int32
ALU = mybir.AluOpType
ACT = mybir.ActivationFunctionType
AX_X = mybir.AxisListType.X
RMAX = bass.bass_isa.ReduceOp.max

P = 128
WIN = 128
KEEP, ALPHA, HOPS = 0.33, 0.7, 2
NEG = 10000.0
LN_EPS, DIV_EPS = 1e-5, 1e-6
MASK_UNIT = 200.0
BOUND_MAX = 32.0
CH = 512
TC = CH // P


def kernel_program(nc, x, Wq, Wk, Wv, Wo, w1, b1, w2, b2, out):
    B, S, D = x.shape
    F = w1.shape[0]
    T = S // P
    NC = S // CH
    KD = D // P
    FT = F // P
    H, HD = 16, D // 16
    KVH = Wk.shape[1] // HD
    REP = H // KVH
    QT = H * HD // P
    HT = P // HD
    NQ = 4
    NPART = 6
    QPART = [0, 1, 2, 0, 1, 0]
    KPART = [0, 0, 0, 1, 1, 2]
    KROWS = NPART * HD
    SHIFT_ROWS = 3
    KEEPN = max(1, int(KEEP * S))
    VW = HD + 1
    assert (KD, QT, NC, T, KVH * HD) == (2, 2, 2, 8, P)

    STEPS = [(c, g, kb) for c in range(NC) for g in range(H // NQ) for kb in range(TC * (c + 1))]
    NSTEP = len(STEPS)
    NG = NC * H // NQ
    GROUP_END = [max(i for i, (c, g, _) in enumerate(STEPS) if c * (H // NQ) + g == n) for n in range(NG)]
    C1 = GROUP_END[H // NQ - 1] + 1
    NHID = 3
    LAG = 2

    def has_tri(i):
        return STEPS[i][2] >= TC * STEPS[i][0]

    def has_local(i):
        c, _, kb = STEPS[i]
        return TC * c <= kb + 1 < TC * (c + 1)

    def spans(i):
        c, _, kb = STEPS[i]
        lo = P * max(0, kb - TC * c)
        return lo, min(CH, max(lo, P * (kb + 2 - TC * c)))

    with ExitStack() as ctx:
        def sb(name, shape, dt=F32):
            return ctx.enter_context(nc.sbuf_tensor(name, shape, dt))

        def sem(name):
            s = ctx.enter_context(nc.semaphore(name))
            sems.append(s)
            return s

        sems = []
        ident = sb("ident", [P, P])
        ones = sb("ones", [P, P])
        before = sb("before", [P, P], BF16)
        after = sb("after", [P, P], BF16)
        band = sb("band", [P, 3, P], BF16)
        w1T = sb("w1T", [P, KD, F], F32R)
        w2T = sb("w2T", [P, FT, D], F32R)
        NW = 2 * D
        wqkv_hi = sb("wqkv_hi", [P, KD, NW], F32R)
        wqkv_lo = sb("wqkv_lo", [P, KD, NW], F32R)
        wo_sb = sb("wo_sb", [P, KD, D])
        b1_sb = sb("b1_sb", [P, FT])
        b2_bc = sb("b2_bc", [P, D])
        wsum = sb("wsum", [P, 2, T + 1])
        thr = sb("thr", [P, 2, 2])
        bound = sb("bound", [P, 8])
        shift = sb("shift", [P, 1])
        exact_flag = sb("exact_flag", [P, 1], I32)
        xn = sb("xn", [P, T, D])
        xT_hi = sb("xT_hi", [P, KD, S], F32R)
        xT_lo = sb("xT_lo", [P, KD, S], F32R)
        q_parts = sb("q_parts", [P, QT, 3, S], BF16)
        k_parts = sb("k_parts", [P, 3, S], BF16)
        q_stack = sb("q_stack", [P, H, S], BF16)
        k_stack = sb("k_stack", [P, KVH, S], BF16)
        v_sb = sb("v_sb", [P, T, KVH * VW + 32 - VW])
        probs = sb("probs", [P, 3, NQ, CH])
        near_mask = sb("near_mask", [P, T, P], BF16)
        mask_ident = sb("mask_ident", [P, P], BF16)
        key_bias = sb("key_bias", [P, T])
        landmark = sb("landmark", [P, T])
        hid = sb("hid", [P, NHID, CH])
        h_hi = sb("h_hi", [P, FT, CH], F32R)
        h_lo = sb("h_lo", [P, FT, CH], F32R)
        gate = sb("gate", [P, TC, D])
        prod = sb("prod", [P, D])
        att_raw = sb("att_raw", [P, CH])
        attT = sb("attT", [P, QT, CH])
        den = sb("den", [P, P])
        rden = den
        rden_bc = sb("rden_bc", [P, QT, CH])
        resid = sb("resid", [P, CH])
        stats = sb("stats", [P, T, 6])
        mv = sb("mv", [P, T, 2])
        root_in = sb("root_in", [P, T + 1])
        root = sb("root", [P, T + 1])
        root_t = sb("root_t", [P, T + 1])
        rstd = sb("rstd", [P, T])
        ssq = sb("ssq", [P, T + 1])
        norm = sb("norm", [P, T + 1])
        dots = sb("dots", [P, T])
        score = sb("score", [P, T])
        score_t = sb("score_t", [P, T])
        count = sb("count", [P, T, 4])
        lm_pad = sb("lm_pad", [P, T + 2], BF16)
        score_row = rden_bc[:, :, :].rearrange("p a n -> p (a n)")
        junk = resid[:, :].bitcast(BF16)
        mean_row = prod
        w1_nat = probs[:, 0].rearrange("p a n -> p (a n)").rearrange("p (t d) -> p t d", d=D)
        w2_nat = probs[:, 1].rearrange("p a n -> p (a n)").rearrange("p (t f) -> p t f", f=F)
        x_prev = hid[:, :, :].rearrange("p a n -> p (a n)")[:, 0:TC * D].rearrange("p (t d) -> p t d", d=D)
        head_block = x_prev[:, 0, 0:P]
        w_tmp = probs[:, 2].rearrange("p a n -> p (a n)")
        scratch = q_parts[:, :, :, :].rearrange("p a b n -> p (a b n)").bitcast(F32)
        w_nat = scratch[:, 0:KD * NW].rearrange("p (k n) -> p k n", k=KD)
        wk_rep = scratch[:, KD * NW:KD * NW + KD * D].rearrange("p (k n) -> p k n", k=KD)
        gram = scratch[:, KD * (NW + D):KD * (NW + D) + D]

        sc_ps = ctx.enter_context(nc.psum_tensor("sc_ps", [P, 4, CH], F32))
        att_ps = ctx.enter_context(nc.psum_tensor("att_ps", [P, 2, CH], F32))
        aux_ps = ctx.enter_context(nc.psum_tensor("aux_ps", [P, 2, CH], F32))

        dve_chain, act_chain, pool_chain = sem("dve_chain"), sem("act_chain"), sem("pool_chain")
        w1_in, w2_in, wqkv_in, wo_in, b_in, x_in = (sem(n) for n in ("w1_in", "w2_in", "wqkv_in", "wo_in", "b_in", "x_in"))
        consts_done, wabs_done, wtotal_done, tern_done, wT_done = (
            sem(n) for n in ("consts_done", "wabs_done", "wtotal_done", "tern_done", "wT_done"))
        wnat_split, gram_done, gram_sum_done, bound_sum_done, bound_ps_done, bound_max_done, bound_root_done = (
            sem(n) for n in ("wnat_split", "gram_done", "gram_sum_done", "bound_sum_done", "bound_ps_done",
                             "bound_max_done", "bound_root_done"))
        aux_done = sem("aux_done")
        aux_free = [sem("aux_free0"), sem("aux_free1")]
        aux_first = sem("aux_first")
        var_done, std_root, xn_done, xT_done = (sem(n) for n in ("var_done", "std_root", "xn_done", "xT_done"))
        dots_done, score_done, row_done, lm_done = (
            sem(n) for n in ("dots_done", "score_done", "row_done", "lm_done"))
        stack_in = [sem("stack_in0"), sem("stack_in1")]
        kstack_in, q_split = sem("kstack_in"), sem("q_split")
        sc_done, exp_done, pv_done = (sem(n) for n in ("sc_done", "exp_done", "pv_done"))
        att_out, att_in, rden_done, rden_in, attT_done = (
            sem(n) for n in ("att_out", "att_in", "rden_done", "rden_in", "attT_done"))
        hid_split, hi_done, hid_split_pool, z_done, gate_done, prod_done, y_done, xres_in, y_out = (
            sem(n) for n in ("hid_split", "hi_done", "hid_split_pool", "z_done", "gate_done", "prod_done", "y_done", "xres_in", "y_out"))
        xprev_in = sem("xprev_in")

        masked_done, max_done, max_row_done, max_split, max_in = (
            sem(n) for n in ("masked_done", "max_done", "max_row_done", "max_split", "max_in"))

        def link(eng, chain, counter):
            def f(ins):
                counter[0] += 1
                ins.then_inc(chain, 1)
                eng.wait_ge(chain, counter[0])
            return f

        def clear_semaphores():
            with nc.Block(no_gpsimd_drain=True) as block:
                @block.sync
                def _(sp):
                    lo = min(s.num for s in sems)
                    assert [s.num for s in sems] == list(range(lo, lo + len(sems)))
                    sp.sem_clear(range(lo, lo + len(sems)))

        with nc.Block(no_gpsimd_drain=True) as block:
            @block.sync
            def _(sp):
                sp.dma_start(w1_nat, w1.rearrange("(t p) d -> p t d", p=P)).then_inc(w1_in, 16)
                sp.dma_start(w2_nat, w2.rearrange("(t p) f -> p t f", p=P)).then_inc(w2_in, 16)
                sp.dma_start(b1_sb[:, :], b1.rearrange("(t p) -> p t", p=P), allow_slow_non_contiguous=True).then_inc(b_in, 16)
                sp.dma_start(b2_bc[0:1, :], b2.rearrange("(a n) -> a n", a=1)).then_inc(b_in, 16)
                sp.wait_ge(b_in, 32)
                sp.wait_ge(x_in, 16)

            @block.scalar
            def _(act):
                act.dma_start(w_nat[:, :, 0:D], Wq.rearrange("(k p) n -> p k n", p=P)).then_inc(wqkv_in, 16)
                act.dma_start(w_nat[:, :, D:D + P], Wk.rearrange("(k p) n -> p k n", p=P)).then_inc(wqkv_in, 16)
                act.dma_start(w_nat[:, :, D + P:NW], Wv.rearrange("(k p) n -> p k n", p=P)).then_inc(wqkv_in, 16)
                act.dma_start(wo_sb[:, :, :], Wo.rearrange("(k p) n -> p k n", p=P)).then_inc(wo_in, 16)
                act.dma_start(xn[:, :, :], x[0].rearrange("(t p) d -> p t d", p=P)).then_inc(x_in, 16)
                for n in range(2 * KD * FT // TC):
                    act.wait_ge(wT_done, n + 1)
                    bank = [sc_ps, att_ps, aux_ps][min(n // 2, 2) if n >= 4 else 0]
                    src = sc_ps[:, n, :] if n < 4 else (att_ps[:, n - 4, :] if n < 6 else aux_ps[:, n - 6, :])
                    if n < 4:
                        dst = w1T[:, n // 2, (n % 2) * CH:(n % 2 + 1) * CH]
                    else:
                        dst = w2T[:, 2 * (n - 4):2 * (n - 3), :].rearrange("p t d -> p (t d)")
                    last = act.activation(dst, src, ACT.Copy)
                last.then_inc(tern_done, 1)
                act.wait_ge(bound_max_done, 2)
                act.activation(bound[:, 5:6], bound[:, 4:5], ACT.Sqrt).then_inc(bound_root_done, 1)
                act.wait_ge(wo_in, 16)

            @block.gpsimd
            def _(pool):
                lk = link(pool, pool_chain, [0])
                for t, v in ((ident, 0.0), (ones, 1.0), (before, 1.0), (after, 1.0), (hid, 1.0),
                             (band, 1.0), (mask_ident, 0.0), (v_sb, 0.0), (lm_pad, 0.0), (count, 0.0), (den, 1.0)):
                    last = pool.memset(t[tuple(slice(None) for _ in t.shape)], v)
                lk(last)

                def select(m, pattern, op, base, mult, fill):
                    lk(pool.affine_select(out=m, in_=m, compare_op=op, fill=fill, base=base,
                                          pattern=pattern, channel_multiplier=mult))
                select(ident[:, :], [[-1, P]], ALU.not_equal, 0, 1, 1.0)
                select(before[:, :], [[-1, P]], ALU.is_gt, 0, 1, 0.0)
                select(after[:, :], [[1, P]], ALU.is_gt, 0, -1, 0.0)
                select(mask_ident[:, :], [[-1, P]], ALU.not_equal, 0, 1, -MASK_UNIT)
                hb = head_block.rearrange("p (g d) -> p g d", d=HD)
                select(hb, [[-HD, HT], [0, HD]], ALU.is_ge, 0, 1, 0.0)
                select(hb, [[HD, HT], [0, HD]], ALU.is_ge, HD - 1, -1, 0.0)
                select(band[:, 0, :], [[-1, P]], ALU.is_ge, HOPS - P, 1, 0.0)
                select(band[:, 1, :], [[-1, P]], ALU.is_ge, HOPS, 1, 0.0)
                select(band[:, 1, :], [[1, P]], ALU.is_ge, HOPS, -1, 0.0)
                select(band[:, 2, :], [[1, P]], ALU.is_ge, HOPS - P, -1, 0.0)
                pool.wait_ge(b_in, 32)
                pool.partition_broadcast(b2_bc[:, :], b2_bc[0:1, :]).then_inc(consts_done, 1)
                lk(pool.memset(v_sb[:, :, 0:KVH * VW].rearrange("p t (j w) -> p t j w", w=VW)[:, :, :, HD:VW], 1.0))
                lk(pool.memset(q_stack[KROWS:KROWS + 32, :, :], 0.0))
                lk(pool.memset(k_stack[KROWS:KROWS + 32, :, :], 1.0))
                pool.wait_ge(bound_sum_done, 1)
                lk(pool.partition_all_reduce(bound[:, 2:4], bound[:, 0:2], P, RMAX))
                pool.sem_inc(bound_max_done, 1)

            @block.vector
            def _(dve):
                lk = link(dve, dve_chain, [0])
                for n, (nat, s) in enumerate(((w1_nat, w1_in), (w2_nat, w2_in))):
                    dve.wait_ge(s, 16)
                    v = nat if n == 0 else nat.rearrange("p t f -> p (t f)").rearrange("p (t d) -> p t d", d=D)
                    lk(dve.tensor_reduce(wsum[:, n, 0:T], v, AX_X, ALU.add, apply_absolute_value=True))
                    dve.tensor_reduce(wsum[:, n, T:T + 1], wsum[:, n, 0:T], AX_X, ALU.add).then_inc(wabs_done, 1)
                dve.wait_ge(wqkv_in, 48)
                for lo in range(0, NW, P):
                    for k in range(KD):
                        src = w_nat[:, k, lo:lo + P]
                        hi, low = wqkv_hi[:, k, lo:lo + P], wqkv_lo[:, k, lo:lo + P]
                        if lo < D + P:
                            src = src.rearrange("p (h d) -> p h d", d=HD)
                            hi, low = (v.rearrange("p (d h) -> p h d", d=HD) for v in (hi, low))
                        lk(dve.tensor_copy(hi, src))
                        lk(dve.tensor_tensor(low, src, hi.bitcast(F32), ALU.subtract))
                for k in range(KD):
                    for r in range(REP):
                        last = dve.tensor_copy(wk_rep[:, k, :].rearrange("p (j r d) -> p j r d", j=KVH, r=REP)[:, :, r, :],
                                               w_nat[:, k, D:D + P].rearrange("p (j d) -> p j d", j=KVH))
                last.then_inc(wnat_split, 1)
                dve.wait_ge(wtotal_done, 1)
                lk(dve.tensor_scalar(thr[:, :, 0], aux_ps[:, 0, 0:2], 1.0 / (F * D), 0.7, ALU.mult, ALU.mult))
                lk(dve.tensor_scalar(thr[:, :, 1], thr[:, :, 0], -1.0, None, ALU.mult))
                for n, nat in enumerate((w1_nat, w2_nat)):
                    flat = nat.rearrange("p a n -> p (a n)")
                    lk(dve.tensor_scalar(w_tmp, flat, thr[:, n, 1:2], None, ALU.is_le))
                    ins = dve.scalar_tensor_tensor(flat, flat, thr[:, n, 0:1], w_tmp, ALU.is_ge, ALU.subtract)
                    ins.then_inc(wabs_done, 1)
                    dve.wait_ge(wabs_done, 3 + n)
                dve.wait_ge(gram_done, 1)
                lk(dve.tensor_copy(gram, aux_ps[:, 1, 0:D]))
                lk(dve.tensor_tensor(gram, gram, aux_ps[:, 1, D:2 * D], ALU.mult))
                for m in range(QT):
                    lk(dve.tensor_tensor(gram[:, m * P:(m + 1) * P], gram[:, m * P:(m + 1) * P], head_block, ALU.mult))
                dve.tensor_reduce(bound[:, 6:8], gram.rearrange("p (m n) -> p m n", n=P), AX_X, ALU.add).then_inc(gram_sum_done, 1)
                dve.wait_ge(bound_ps_done, 1)
                dve.tensor_copy(bound[:, 0:2], aux_ps[:, 0, 8:10]).then_inc(bound_sum_done, 1)
                dve.wait_ge(bound_max_done, 1)
                dve.tensor_reduce(bound[:, 4:5], bound[:, 2:4], AX_X, ALU.max).then_inc(bound_max_done, 1)
                dve.wait_ge(bound_root_done, 1)
                lk(dve.tensor_scalar(bound[:, 6:7], bound[:, 5:6], 1.001 * D / HD ** 0.5, None, ALU.mult))
                lk(dve.tensor_scalar(bound[:, 7:8], bound[:, 6:7], BOUND_MAX, None, ALU.is_le))
                lk(dve.tensor_scalar(exact_flag[:, :], bound[:, 7:8], -1.0, 1.0, ALU.mult, ALU.add))
                lk(dve.tensor_scalar(bound[:, 6:7], bound[:, 6:7], BOUND_MAX, -1.0, ALU.min, ALU.mult))
                lk(dve.tensor_tensor(shift[:, :], bound[:, 6:7], bound[:, 7:8], ALU.mult))

            @block.tensor
            def _(pe):
                pe.wait_ge(consts_done, 1)
                pe.wait_ge(wabs_done, 2)
                pe.matmul(aux_ps[:, 0, 0:2], ones[:, :], wsum[:, :, T], start=True, stop=True).then_inc(wtotal_done, 1)
                pe.wait_ge(wnat_split, 1)
                for n, w in enumerate((w_nat, wk_rep)):
                    for m in range(QT):
                        for k in range(KD):
                            last = pe.matmul(aux_ps[:, 1, (QT * n + m) * P:(QT * n + m + 1) * P], w[:, k, m * P:(m + 1) * P],
                                             w[:, k, m * P:(m + 1) * P], start=(k == 0), stop=(k == KD - 1))
                last.then_inc(gram_done, 1)
                for n in range(2 * KD * FT // TC):
                    if n in (0, 4):
                        pe.wait_ge(wabs_done, 3 + n // 4)
                    if n == 6:
                        pe.wait_ge(gram_sum_done, 1)
                        pe.matmul(aux_ps[:, 0, 8:10], head_block, bound[:, 6:8], start=True, stop=True).then_inc(bound_ps_done, 1)
                        pe.wait_ge(bound_sum_done, 1)
                    dst = sc_ps[:, n, :] if n < 4 else (att_ps[:, n - 4, :] if n < 6 else aux_ps[:, n - 6, :])
                    for q in range(TC):
                        if n < 4:
                            src = w1_nat[:, (n % 2) * TC + q, (n // 2) * P:(n // 2 + 1) * P]
                        else:
                            f = 2 * (n - 4) + q // 2
                            src = w2_nat[:, q % 2, f * P:(f + 1) * P]
                        last = pe.transpose(dst[:, q * P:(q + 1) * P], src, ident[:, :])
                    last.then_inc(wT_done, 1)
        clear_semaphores()

        def row_maxima():
            flat = [probs[:, i].rearrange("p a n -> p (a n)") for i in range(3)]
            key_at, mask = flat[0][:, 0:S], flat[0][:, S:2 * S]
            masked, landmark_row = flat[1][:, 0:S], flat[1][:, S:2 * S]
            row_max, query_at, behind = flat[2][:, 0:H], flat[2][:, H:H + 1], flat[2][:, H + 1:H + 2]
            left = flat[2][0:H, P:2 * P]
            parts = flat[2][0:H, 2 * P:4 * P].bitcast(BF16)[:, 0:3 * P].rearrange("h (r n) -> h r n", r=3)

            with nc.Block(no_gpsimd_drain=True) as block:
                @block.sync
                def _(sp):
                    for i in range(NPART):
                        for m in range(QT):
                            sp.dma_start(q_stack[i * HD:(i + 1) * HD, m * HT:(m + 1) * HT, CH:S],
                                         q_parts[:, m, QPART[i], CH:S]).then_inc(stack_in[1], 16)
                    sp.wait_ge(stack_in[1], 16 * NPART * QT)

                @block.gpsimd
                def _(pool):
                    pool.iota(key_at, [[1, S]], base=0, channel_multiplier=0, allow_small_or_imprecise_dtypes=True)
                    pool.iota(query_at, [[1, 1]], base=0, channel_multiplier=1, allow_small_or_imprecise_dtypes=True)

                @block.tensor
                def _(pe):
                    for t in range(T):
                        last = pe.transpose(sc_ps[:, t // TC, (t % TC) * P:(t % TC + 1) * P],
                                            landmark[:, t:t + 1].to_broadcast([P, P]), ident[:, :])
                    last.then_inc(row_done, 1)

                @block.vector
                def _(dve):
                    dve.memset(q_stack[KROWS:P, :, :], 0.0)

                @block.scalar
                def _(act):
                    act.wait_ge(row_done, 1)
                    act.activation(landmark_row, sc_ps[:, 0:NC, :].rearrange("p a n -> p (a n)"), ACT.Copy)
            clear_semaphores()

            with nc.Fori(0, T) as t:
                with nc.Block(no_gpsimd_drain=True) as block:
                    @block.tensor
                    def _(pe):
                        for h in range(H):
                            if h >= 2:
                                pe.wait_ge(masked_done, h - 1)
                            for half in range(NC):
                                last = pe.matmul(sc_ps[:, 2 * (h % 2) + half, :], q_stack[:, h, bass.ds(t * P, P)],
                                                 k_stack[:, h // REP, half * CH:(half + 1) * CH], start=True, stop=True)
                            last.then_inc(sc_done, 1)
                        pe.wait_ge(max_done, 1)
                        pe.transpose(aux_ps[0:H, 0, 0:P], row_max, ident[:, :]).then_inc(max_row_done, 1)

                    @block.vector
                    def _(dve):
                        lk = link(dve, dve_chain, [0])
                        lk(dve.tensor_scalar(behind, query_at, -float(WIN), None, ALU.add))
                        lk(dve.scalar_tensor_tensor(mask, key_at, behind, landmark_row, ALU.is_gt, ALU.max))
                        lk(dve.scalar_tensor_tensor(mask, key_at, query_at, mask, ALU.is_le, ALU.mult))
                        lk(dve.tensor_scalar(mask, mask, -1.0, NEG * HD ** 0.5, ALU.add, ALU.mult))
                        for h in range(H):
                            dve.wait_ge(sc_done, h + 1)
                            ps = sc_ps[:, 2 * (h % 2):2 * (h % 2) + 2, :].rearrange("p a n -> p (a n)")
                            dve.tensor_tensor(masked, ps, mask, ALU.add).then_inc(masked_done, 1)
                            dve.wait_ge(masked_done, h + 1)
                            lk(dve.tensor_reduce(row_max[:, h:h + 1], masked, AX_X, ALU.max))
                        dve.tensor_scalar(row_max, row_max, -1.0, None, ALU.mult).then_inc(max_done, 1)
                        lk(dve.tensor_scalar(query_at, query_at, float(P), None, ALU.add))
                        dve.wait_ge(aux_first, 1)
                        lk(dve.tensor_tensor(left, aux_ps[0:H, 0, 0:P], parts[:, 0, :], ALU.subtract))
                        lk(dve.tensor_copy(parts[:, 1, :], left))
                        dve.tensor_tensor(parts[:, 2, :], left, parts[:, 1, :], ALU.subtract).then_inc(max_split, 1)

                    @block.scalar
                    def _(act):
                        act.wait_ge(max_row_done, 1)
                        act.activation(parts[:, 0, :], aux_ps[0:H, 0, 0:P], ACT.Copy).then_inc(aux_first, 1)

                    @block.sync
                    def _(sp):
                        sp.wait_ge(max_split, 1)
                        for r in range(SHIFT_ROWS):
                            sp.dma_start(q_stack[KROWS + r:KROWS + r + 1, :, bass.ds(t * P, P)],
                                         parts[:, r, :]).then_inc(max_in, 16)
                        sp.wait_ge(max_in, 16 * SHIFT_ROWS)
                clear_semaphores()

        FFN_DOWN_AT = (6, 7, 9, 10, 11, 12, 13, 14)
        DOTS_AT, RANK_AT = 6, 19
        LN_AT = 5

        def jobs_of(main, prep, prev):
            jobs = []
            n_prev = TC if prev else 0
            if prev:
                jobs += [(4 + t // 2, "out_proj", TC + t, t) for t in range(TC)]
            if main:
                jobs += [(at, "ffn_down", i // 2, i % 2) for i, at in enumerate(FFN_DOWN_AT)]
                jobs += [(C1 - 0.5, "ffn_up", 1, f, f) for f in range(FT)]
                jobs += [(C1 + at, "out_proj", t, n_prev + t) for t, at in enumerate((11, 13, 15, 16))]
                jobs += [(C1 + 18 + 2 * t + half, "ffn_down", TC + t, half) for t in range(TC) for half in range(2)]
            if main and not prep:
                jobs += [(NSTEP + 5, "out_proj", TC + t, n_prev + TC + t) for t in range(TC)]
            if prep:
                s = C1 if main else 0
                jobs += [(s + 1 + KD * c + k, "transpose", k, c) for c in range(NC) for k in range(KD)]
                jobs += [(s + 5 + c, "k_proj", c) for c in range(NC)]
                jobs += [(s - 0.4 if main else 0, "mean_row")]
                jobs += [(s + at, "q_proj", m, c) for (m, c), at in zip(((0, 0), (1, 0), (0, 1), (1, 1)), (8, 10, 12, 14))]
                jobs += [(s + 17, "score_row", i) for i in range(2)]
                jobs += [(s + 28, "dilate")]
                if main:
                    jobs += [(NSTEP + 3, "v_proj", i) for i in range(2)]
                    jobs += [(NSTEP + (0 if f < 2 else LAG), "ffn_up", 0, f, FT + f) for f in range(FT)]
                else:
                    jobs += [(16, "v_proj", i) for i in range(2)]
                    jobs += [(RANK_AT + f, "ffn_up", 0, f, f) for f in range(FT)]
            return sorted(jobs, key=lambda j: j[0])

        def turn(b, main, prep, prev, x_next):
            if main:
                with nc.If(exact != 0):
                    row_maxima()
            jobs = jobs_of(main, prep, prev)
            n_prev = TC if prev else 0
            S0 = C1 if main else 0
            last_step = RANK_AT + T + 1

            def jobs_at(lo, hi):
                return [(n,) + j[1:] for n, j in enumerate(jobs) if lo <= j[0] < hi]

            bank_of, used = [], [0, 0]
            for j in jobs:
                if j[1] == "ffn_down" and j[3]:
                    bank_of.append(bank_of[-1])
                    continue
                bank = sum(used) % 2
                bank_of.append((bank, used[bank]))
                used[bank] += 1

            n_transposes = [n for n, j in enumerate(jobs) if j[1] == "transpose"]

            with nc.Block(no_gpsimd_drain=True) as block:
                @block.sync
                def _(sp):
                    def stack_q(c):
                        cs = slice(c * CH, (c + 1) * CH)
                        for i in range(NPART):
                            for m in range(QT):
                                sp.dma_start(q_stack[i * HD:(i + 1) * HD, m * HT:(m + 1) * HT, cs],
                                             q_parts[:, m, QPART[i], cs]).then_inc(stack_in[c], 16)

                    def stack_k():
                        for i in range(NPART):
                            sp.dma_start(k_stack[i * HD:(i + 1) * HD, :, :], k_parts[:, KPART[i], :]).then_inc(kstack_in, 16)

                    def att_group(n):
                        c, g = n // (H // NQ), n % (H // NQ)
                        sp.wait_ge(att_out, n + 1)
                        if g == 0 and (c == 1 or prev):
                            sp.wait_ge(aux_done, 1 + [i for i, j in enumerate(jobs) if j[1] == "out_proj"][n_prev - 1 + c * TC])
                        h = g * NQ
                        for q in range(NQ):
                            row = (h % HT + q) * HD
                            sp.dma_start(attT[row:row + HD, h // HT, :], att_raw[32 * q:32 * q + HD, :]).then_inc(att_in, 16)
                        sp.dma_start(den[h * TC:(h + NQ) * TC, :], att_raw[HD:P:32, :]).then_inc(att_in, 16)

                    def spread_rden(turn_no):
                        sp.wait_ge(rden_done, turn_no + 1)
                        for m in range(QT):
                            for s in range(TC):
                                src = rden[m * HT * TC + s:(m + 1) * HT * TC:TC, :]
                                sp.dma_start(rden_bc[:, m, s * P:(s + 1) * P],
                                             src.unsqueeze(1).to_broadcast([HT, HD, P])).then_inc(rden_in, 16)

                    if main:
                        xb = x[b].rearrange("(t p) d -> p t d", p=P)
                        ob = out[b].rearrange("(t p) d -> p t d", p=P)
                        if prev:
                            xp = x[b - 1].rearrange("(t p) d -> p t d", p=P)
                            op = out[b - 1].rearrange("(t p) d -> p t d", p=P)
                            spread_rden(0)
                            sp.dma_start(x_prev[:, :, :], xp[:, TC:T, :]).then_inc(xprev_in, 16)
                        if prep:
                            sp.dma_start(xn[:, :, :], x_next.rearrange("(t p) d -> p t d", p=P)).then_inc(x_in, 16)
                        stack_q(1)
                        if prev:
                            sp.wait_ge(y_done, TC)
                            sp.dma_start(op[:, TC:T, :], x_prev[:, :, :]).then_inc(y_out, 16)
                        for n in range(4):
                            att_group(n)
                        spread_rden(int(prev))
                        x_end = TC if prep else T
                        if prep:
                            sp.wait_ge(aux_done, n_transposes[-1] + 1)
                            sp.wait_ge(dots_done, T)
                        sp.dma_start(xn[:, 0:x_end, :], xb[:, 0:x_end, :]).then_inc(xres_in, 16)
                        att_group(4)
                        if prep:
                            sp.wait_ge(q_split, 2)
                            stack_q(0)
                        att_group(5)
                        sp.wait_ge(y_done, n_prev + TC)
                        sp.dma_start(ob[:, 0:TC, :], xn[:, 0:TC, :]).then_inc(y_out, 16)
                        att_group(6)
                        if prep:
                            sp.wait_ge(sc_done, 2 * NSTEP)
                            stack_k()
                        att_group(7)
                        if prep:
                            sp.wait_ge(att_in, 16 * (NQ + 1) * NG)
                        else:
                            spread_rden(prev + 1)
                            sp.wait_ge(y_done, n_prev + 2 * TC)
                            sp.dma_start(ob[:, TC:T, :], xn[:, TC:T, :]).then_inc(y_out, 16)
                        sp.wait_ge(y_out, 16 * (prev + 1 + (not prep)))
                    else:
                        sp.wait_ge(q_split, QT * NC)
                        stack_k()
                        stack_q(0)
                    if prep:
                        sp.wait_ge(hid_split_pool, (1 + main) * FT // 2)
                        sp.wait_ge(stack_in[0], 16 * NPART * QT)
                        sp.wait_ge(kstack_in, 16 * NPART)

                @block.tensor
                def _(pe):
                    def job(n, kind, *a):
                        bank, before_it = bank_of[n]
                        ps = aux_ps[:, bank, :]
                        if before_it and not (kind == "ffn_down" and a[1]):
                            pe.wait_ge(aux_free[bank], before_it)
                        if kind == "ffn_up":
                            c, f, _ = a
                            for k in range(KD):
                                for part in (xT_hi, xT_lo):
                                    last = pe.matmul(ps, w1T[:, k, f * P:(f + 1) * P], part[:, k, c * CH:(c + 1) * CH],
                                                     start=(k == 0 and part is xT_hi), stop=(k == KD - 1 and part is xT_lo))
                        elif kind == "ffn_down":
                            t, half = a
                            if t >= TC:
                                pe.wait_ge(hid_split, FT // 2)
                                pe.wait_ge(hid_split_pool, FT // 2)
                            q = t % TC
                            for f in range(half * FT // 2, (half + 1) * FT // 2):
                                for part in (h_hi, h_lo):
                                    last = pe.matmul(ps[:, 0:D], part[:, f, q * P:(q + 1) * P], w2T[:, f, :],
                                                     start=(f == 0 and part is h_hi), stop=(f == FT - 1 and part is h_lo))
                        elif kind == "out_proj":
                            t, u = a
                            pe.wait_ge(attT_done, u // TC + 1)
                            q = t % TC
                            for k in range(KD):
                                last = pe.matmul(ps[:, 0:D], attT[:, k, q * P:(q + 1) * P], wo_sb[:, k, :],
                                                 start=(k == 0), stop=(k == KD - 1))
                        elif kind == "transpose":
                            k, c = a
                            pe.wait_ge(xn_done, TC * (c + 1))
                            for q in range(TC):
                                last = pe.transpose(ps[:, q * P:(q + 1) * P], xn[:, c * TC + q, k * P:(k + 1) * P], ident[:, :])
                        elif kind in ("k_proj", "q_proj"):
                            m, c = a if kind == "q_proj" else (QT, a[0])
                            pe.wait_ge(xT_done, KD * NC)
                            ws, xs = slice(m * P, (m + 1) * P), slice(c * CH, (c + 1) * CH)
                            mms = [(w, xp, k) for k in range(KD) for w, xp in ((wqkv_hi, xT_hi), (wqkv_hi, xT_lo), (wqkv_lo, xT_hi))]
                            for i, (w, xp, k) in enumerate(mms):
                                last = pe.matmul(ps, w[:, k, ws], xp[:, k, xs], start=(i == 0), stop=(i == len(mms) - 1))
                        elif kind == "v_proj":
                            for q in range(TC):
                                t = a[0] * TC + q
                                mms = [(xp, w, k) for k in range(KD) for xp, w in ((xT_hi, wqkv_hi), (xT_lo, wqkv_hi), (xT_hi, wqkv_lo))]
                                for i, (xp, w, k) in enumerate(mms):
                                    last = pe.matmul(ps[:, q * P:(q + 1) * P], xp[:, k, t * P:(t + 1) * P], w[:, k, D + P:NW],
                                                     start=(i == 0), stop=(i == len(mms) - 1))
                        elif kind == "mean_row":
                            pe.wait_ge(xn_done, T)
                            for t in range(T):
                                last = pe.matmul(ps[:, 0:D], ones[:, :], xn[:, t, :], start=(t == 0), stop=(t == T - 1))
                        elif kind == "score_row":
                            pe.wait_ge(score_done, 1)
                            for q in range(TC):
                                t = a[0] * TC + q
                                last = pe.transpose(ps[:, q * P:(q + 1) * P], score[:, t:t + 1].to_broadcast([P, P]), ident[:, :])
                        elif kind == "dilate":
                            pe.wait_ge(lm_done, 1)
                            for i in range(3):
                                last = pe.matmul(ps[:, 0:T], band[:, i, :], lm_pad[:, i:i + T], start=(i == 0), stop=(i == 2))
                        last.then_inc(aux_done, 1)

                    def scores(i, u):
                        c, g, kb = STEPS[i]
                        if i == C1 and u == 0:
                            pe.wait_ge(stack_in[1], 16 * NPART * QT)
                        lo, near = spans(i)
                        if True:
                            if i >= 1:
                                pe.wait_ge(exp_done, 2 * (i - 1) + u + 1)
                            for hh in range(2):
                                h = g * NQ + 2 * u + hh
                                last = pe.matmul(sc_ps[:, 2 * u + hh, lo:CH], k_stack[0:KROWS + SHIFT_ROWS, h // REP, kb * P:(kb + 1) * P],
                                                 q_stack[0:KROWS + SHIFT_ROWS, h, c * CH + lo:(c + 1) * CH], start=True, stop=(near == lo))
                            if near > lo:
                                first = 0 if has_tri(i) else kb + 1
                                end = kb + 2 if has_local(i) else 1
                                for hh in range(2):
                                    last = pe.matmul(sc_ps[:, 2 * u + hh, lo:near], mask_ident[:, :], near_mask[:, first:end:kb + 1, :],
                                                     start=False, stop=True)
                            last.then_inc(sc_done, 1)

                    def values(i):
                        c, g, kb = STEPS[i]
                        n = c * (H // NQ) + g
                        if kb == 0 and n >= 2:
                            pe.wait_ge(att_out, n - 1)
                        pe.wait_ge(exp_done, 2 * (i + 1))
                        lo = spans(i)[0]
                        for q in range(NQ):
                            j = (g * NQ + q) // REP
                            last = pe.matmul(att_ps[32 * q:32 * q + 32, n % 2, lo:CH], v_sb[:, kb, j * VW:j * VW + 32],
                                             probs[:, i % 3, q, lo:CH], start=(kb == 0), stop=(kb == TC * (c + 1) - 1))
                        last.then_inc(pv_done, 1)

                    if main:
                        for i in range(NSTEP + LAG):
                            for j in jobs_at(i - 0.5, i):
                                job(*j)
                            if i < NSTEP:
                                scores(i, 0)
                            if i >= LAG:
                                values(i - LAG)
                            if i < NSTEP:
                                scores(i, 1)
                            for j in jobs_at(i, i + 0.5):
                                job(*j)
                        for j in jobs_at(NSTEP + LAG - 0.5, 999):
                            job(*j)
                    else:
                        for j in jobs_at(0, 999):
                            job(*j)

                @block.scalar
                def _(act):
                    def job(n, kind, *a):
                        bank, before_it = bank_of[n]
                        ps = aux_ps[:, bank, :]
                        if kind == "ffn_up":
                            c, f, u = a
                            act.wait_ge(aux_done, n + 1)
                            if u >= NHID:
                                act.wait_ge([hid_split, hid_split_pool][(u - NHID) % 2], (u - NHID) // 2 + 1)
                            if u == 0 and prev:
                                act.wait_ge(y_out, 16)
                            act.activation(hid[:, u % NHID, :], ps, ACT.Gelu, bias=b1_sb[:, f:f + 1]).then_inc(aux_free[bank], 1)
                        elif kind == "transpose":
                            k, c = a
                            act.wait_ge(aux_done, n + 1)
                            act.activation(xT_hi[:, k, c * CH:(c + 1) * CH], ps, ACT.Copy).then_inc(aux_first, 1)
                        elif kind in ("k_proj", "q_proj"):
                            dst = k_parts[:, 0, a[0] * CH:(a[0] + 1) * CH] if kind == "k_proj" else \
                                q_parts[:, a[0], 0, a[1] * CH:(a[1] + 1) * CH]
                            act.wait_ge(aux_done, n + 1)
                            if main and kind == "q_proj":
                                act.wait_ge(stack_in[1], 16 * NPART * QT)
                            act.activation(dst, ps, ACT.Copy).then_inc(aux_first, 1)
                        elif kind == "v_proj":
                            act.wait_ge(aux_done, n + 1)
                            for q in range(TC):
                                t = a[0] * TC + q
                                last = act.activation(v_sb[:, t, 0:KVH * VW].rearrange("p (j w) -> p j w", w=VW)[:, :, 0:HD],
                                                      ps[:, q * P:(q + 1) * P].rearrange("p (j d) -> p j d", d=HD), ACT.Copy)
                            last.then_inc(aux_free[bank], 1)
                        elif kind == "score_row":
                            act.wait_ge(aux_done, n + 1)
                            act.activation(score_row[:, a[0] * CH:(a[0] + 1) * CH], ps, ACT.Copy).then_inc(row_done, 1)
                            act.wait_ge(row_done, a[0] + 1)
                            act.sem_inc(aux_free[bank], 1)

                    def gates(c):
                        act.wait_ge(z_done, TC * (c + 1))
                        act.activation(gate[:, :, :], gate[:, :, :], ACT.Silu).then_inc(gate_done, 1)

                    def exps(i):
                        c, g, kb = STEPS[i]
                        lo, near = spans(i)
                        if i >= 3:
                            act.wait_ge(pv_done, i - 2)
                        for u in range(2):
                            act.wait_ge(sc_done, 2 * i + u + 1)
                            us = slice(2 * u, 2 * u + 2)
                            if near > lo:
                                last = act.activation(probs[:, i % 3, us, lo:near], sc_ps[:, us, lo:near], ACT.Exp,
                                                      bias=shift[:, 0:1], scale=HD ** -0.5)
                            if near < CH:
                                last = act.activation(probs[:, i % 3, us, near:CH], sc_ps[:, us, near:CH], ACT.Exp,
                                                      bias=key_bias[:, kb:kb + 1], scale=HD ** -0.5)
                            last.then_inc(exp_done, 1)

                    for i in range(NSTEP if main else last_step + 1):
                        for j in jobs_at(i - 0.5, i):
                            job(*j)
                        if main and i == C1:
                            gates(0)
                        if main:
                            exps(i)
                        for j in jobs_at(i, i + 0.5):
                            job(*j)
                    if main:
                        tail = jobs_at(NSTEP - 0.5, 999)
                        first = [j for j in tail if j[1] == "ffn_up"]
                        for j in first:
                            job(*j)
                        gates(1)
                        for j in tail[len(first):]:
                            job(*j)

                @block.gpsimd
                def _(pool):
                    def residual(t, u):
                        if u == 0 and prev:
                            pool.wait_ge(xprev_in, 16)
                        if u == n_prev:
                            pool.wait_ge(xres_in, 16)
                        pool.wait_ge(prod_done, u + 1)
                        x_tile = x_prev[:, t - TC, :] if u < n_prev else xn[:, t, :]
                        pool.tensor_tensor(x_tile, x_tile, prod[:, :], ALU.add).then_inc(y_done, 1)

                    def split_rest(f, u):
                        pool.wait_ge(hi_done, u // 2 + 1)
                        pool.tensor_tensor(h_lo[:, f, :], hid[:, u % NHID, :], h_hi[:, f, :].bitcast(F32),
                                           ALU.subtract).then_inc(hid_split_pool, 1)

                    for _, kind, *a in jobs_at(0, 999):
                        if kind == "out_proj":
                            residual(*a)
                        if kind == "ffn_up" and a[2] % 2:
                            split_rest(*a[1:])

                @block.vector
                def _(dve):
                    lk = link(dve, dve_chain, [0])

                    def rsqrt(m):
                        v, y, t = root_in[:, 0:m], root[:, 0:m], root_t[:, 0:m]
                        lk(dve.tensor_scalar(y.bitcast(I32), v.bitcast(I32), -0.5, 1597463007.0, ALU.mult, ALU.add))
                        lk(dve.tensor_scalar(v, v, -0.5, None, ALU.mult))
                        for _ in range(3):
                            lk(dve.tensor_tensor(t, v, y, ALU.mult))
                            lk(dve.tensor_tensor(t, t, y, ALU.mult))
                            lk(dve.scalar_tensor_tensor(y, t, 1.5, y, ALU.add, ALU.mult))

                    def commit():
                        lk(dve.tensor_scalar(key_bias[:, :], landmark[:, :], -1.0, NEG, ALU.add, ALU.mult))
                        lk(dve.tensor_scalar(key_bias[:, :], key_bias[:, :], shift[:, 0:1], None, ALU.add))
                        lk(dve.tensor_scalar(near_mask[:, 0, :], before[:, :], MASK_UNIT, None, ALU.mult))
                        for t in range(T - 1):
                            last = dve.tensor_scalar(near_mask[:, t + 1, :], before[:, :], landmark[:, t:t + 1], -MASK_UNIT, ALU.max, ALU.mult)
                        lk(last)
                        dve.tensor_scalar(near_mask[:, 1:T, :], near_mask[:, 1:T, :], MASK_UNIT, None, ALU.add)

                    def job(n, kind, *a):
                        bank, before_it = bank_of[n]
                        ps = aux_ps[:, bank, :]
                        if kind == "ffn_up":
                            c, f, u = a
                            dve.wait_ge(aux_free[bank], before_it + 1)
                            whole = hid[:, u % NHID, :]
                            ins = dve.tensor_copy(h_hi[:, f, :], whole)
                            if u % 2:
                                ins.then_inc(hi_done, 1)
                            else:
                                lk(ins)
                                dve.tensor_tensor(h_lo[:, f, :], whole, h_hi[:, f, :].bitcast(F32), ALU.subtract).then_inc(hid_split, 1)
                        elif kind == "ffn_down" and a[1]:
                            t = a[0]
                            dve.wait_ge(aux_done, n + 1)
                            dve.tensor_tensor(gate[:, t % TC, :], ps[:, 0:D], b2_bc[:, :], ALU.add).then_inc(z_done, 1)
                            dve.wait_ge(z_done, t + 1)
                            dve.sem_inc(aux_free[bank], 1)
                        elif kind == "out_proj":
                            t, u = a
                            dve.wait_ge(aux_done, n + 1)
                            if u >= 1:
                                dve.wait_ge(y_done, u)
                            if u >= n_prev and t % TC == 0:
                                dve.wait_ge(gate_done, t // TC + 1)
                            dve.tensor_tensor(prod[:, :], ps[:, 0:D], gate[:, t % TC, :], ALU.mult).then_inc(prod_done, 1)
                            dve.wait_ge(prod_done, u + 1)
                            dve.sem_inc(aux_free[bank], 1)
                        elif kind == "transpose":
                            k, c = a
                            m = c * KD + k
                            dve.wait_ge(aux_first, m + 1)
                            dve.tensor_tensor(xT_lo[:, k, c * CH:(c + 1) * CH], ps,
                                              xT_hi[:, k, c * CH:(c + 1) * CH].bitcast(F32), ALU.subtract).then_inc(xT_done, 1)
                            dve.wait_ge(xT_done, m + 1)
                            dve.sem_inc(aux_free[bank], 1)
                        elif kind in ("k_proj", "q_proj"):
                            first = KD * NC + (a[0] if kind == "k_proj" else NC + a[1] * QT + a[0])
                            c = a[0] if kind == "k_proj" else a[1]
                            part = [(k_parts[:, r, c * CH:(c + 1) * CH] if kind == "k_proj" else
                                     q_parts[:, a[0], r, c * CH:(c + 1) * CH]) for r in range(3)]
                            dve.wait_ge(aux_first, first + 1)
                            ins = dve.tensor_tensor(resid[:, :], ps, part[0], ALU.subtract)
                            ins.then_inc(aux_free[bank], 1)
                            dve.wait_ge(aux_free[bank], before_it + 1)
                            lk(dve.tensor_copy(part[1], resid[:, :]))
                            ins = dve.tensor_tensor(part[2], resid[:, :], part[1], ALU.subtract)
                            if kind == "q_proj":
                                ins.then_inc(q_split, 1)
                                dve.wait_ge(q_split, 1 + QT * c + a[0])
                            else:
                                lk(ins)
                        elif kind == "mean_row":
                            dve.wait_ge(aux_done, n + 1)
                            if n_prev:
                                dve.wait_ge(y_done, n_prev)
                            dve.tensor_scalar(mean_row[:, :], ps[:, 0:D], 1.0 / S, None, ALU.mult).then_inc(aux_free[bank], 1)
                            dve.wait_ge(aux_free[bank], before_it + 1)
                        elif kind == "dilate":
                            dve.wait_ge(aux_done, n + 1)
                            dve.tensor_scalar(landmark[:, :], ps[:, 0:T], 1.0, None, ALU.min).then_inc(aux_free[bank], 1)
                            dve.wait_ge(aux_free[bank], before_it + 1)

                    def layer_norm(k):
                        if k < T:
                            if k == 0 and main:
                                dve.wait_ge(x_in, 16)
                            lk(dve.bn_stats(stats[:, k, :], xn[:, k, :]))
                            lk(dve.bn_aggr(mv[:, k, :], stats[:, k, :]))
                        elif k == T:
                            lk(dve.tensor_scalar(root_in[:, 0:T], mv[:, :, 1], LN_EPS, None, ALU.add))
                            rsqrt(T)
                            lk(dve.tensor_copy(rstd[:, :], root[:, 0:T]))

                    def normalise_x(t):
                        dve.tensor_scalar(xn[:, t, :], xn[:, t, :], mv[:, t, 0:1], rstd[:, t:t + 1], ALU.subtract, ALU.mult).then_inc(xn_done, 1)
                        dve.wait_ge(xn_done, t + 1)
                        lk(dve.scalar_tensor_tensor(resid[:, 0:D], xn[:, t, :], 1.0, xn[:, t, :], ALU.mult, ALU.mult,
                                                    accum_out=ssq[:, t:t + 1]))

                    def token_dot(t):
                        ins = dve.scalar_tensor_tensor(resid[:, 0:D], xn[:, t, :], 1.0, mean_row[:, :], ALU.mult, ALU.mult,
                                                       accum_out=dots[:, t:t + 1])
                        ins.then_inc(dots_done, 1)
                        dve.wait_ge(dots_done, t + 1)

                    def token_scores():
                        lk(dve.scalar_tensor_tensor(resid[:, 0:D], mean_row[:, :], 1.0, mean_row[:, :], ALU.mult, ALU.mult,
                                                    accum_out=ssq[:, T:T + 1]))
                        lk(dve.tensor_copy(root_in[:, :], ssq[:, :]))
                        rsqrt(T + 1)
                        lk(dve.tensor_tensor(norm[:, :], ssq[:, :], root[:, :], ALU.mult))
                        lk(dve.tensor_scalar(root_t[:, 0:T], norm[:, 0:T], norm[:, T:T + 1], DIV_EPS, ALU.mult, ALU.add))
                        lk(dve.reciprocal(root_t[:, 0:T], root_t[:, 0:T]))
                        lk(dve.tensor_tensor(score_t[:, :], dots[:, :], root_t[:, 0:T], ALU.mult))
                        lk(dve.tensor_scalar(score_t[:, :], score_t[:, :], -(1.0 - ALPHA), None, ALU.mult))
                        lk(dve.tensor_scalar(score[:, :], norm[:, 0:T], ALPHA, None, ALU.mult))
                        dve.tensor_tensor(score[:, :], score[:, :], score_t[:, :], ALU.add).then_inc(score_done, 1)

                    def rank(t):
                        if t == 0:
                            dve.wait_ge(score_done, 1)
                            dve.wait_ge(row_done, 2)
                        own, at = score[:, t:t + 1], slice(t * P, (t + 1) * P)
                        if t > 0:
                            dve.tensor_scalar(junk[:, 0:t * P], score_row[:, 0:t * P], own, 0.0, ALU.is_ge, ALU.add,
                                              accum_out=count[:, t, 0:1])
                        if t < T - 1:
                            dve.tensor_scalar(junk[:, (t + 1) * P:S], score_row[:, (t + 1) * P:S], own, 0.0, ALU.is_gt, ALU.add,
                                              accum_out=count[:, t, 1:2])
                        lk(dve.scalar_tensor_tensor(junk[:, at], score_row[:, at], own, before[:, :], ALU.is_ge, ALU.mult,
                                                    accum_out=count[:, t, 2:3]))
                        lk(dve.scalar_tensor_tensor(junk[:, at], score_row[:, at], own, after[:, :], ALU.is_gt, ALU.mult,
                                                    accum_out=count[:, t, 3:4]))
                        if t == T - 1:
                            lk(dve.tensor_reduce(score_t[:, :], count[:, :, :], AX_X, ALU.add))
                            dve.tensor_scalar(lm_pad[:, 1:T + 1], score_t[:, :], float(KEEPN), None, ALU.is_lt).then_inc(lm_done, 1)

                    def group_out(n):
                        dve.wait_ge(pv_done, GROUP_END[n] + 1)
                        if n >= 1:
                            dve.wait_ge(att_in, 16 * (NQ + 1) * n)
                        dve.tensor_copy(att_raw[:, :], att_ps[:, n % 2, :]).then_inc(att_out, 1)

                    def reciprocals(groups):
                        if groups:
                            dve.wait_ge(att_in, 16 * (NQ + 1) * groups)
                        dve.reciprocal(rden[0:H * TC, :], den[0:H * TC, :]).then_inc(rden_done, 1)

                    def normalise_heads(turn_no):
                        dve.wait_ge(rden_in, 16 * QT * TC * (turn_no + 1))
                        dve.tensor_tensor(attT[:, :, :], attT[:, :, :], rden_bc[:, :, :], ALU.mult).then_inc(attT_done, 1)

                    if prev:
                        reciprocals(0)
                    if prep and not main:
                        for k in range(T + 1):
                            layer_norm(k)
                        for k in range(T):
                            normalise_x(k)
                    for i in range(last_step + 1 if not main else NSTEP + LAG):
                        for j in jobs_at(i - 0.5, i):
                            job(*j)
                        for j in jobs_at(i, i + 0.5):
                            job(*j)
                        if main:
                            for n in range(NG):
                                if GROUP_END[n] + LAG == i:
                                    group_out(n)
                            if prev and i == 3:
                                normalise_heads(0)
                            if i == C1 + 5:
                                reciprocals(NG // 2)
                            if i == C1 + 8:
                                normalise_heads(int(prev))
                            if prep and LN_AT <= i < LN_AT + T // 2 + 1:
                                for k in range(2 * (i - LN_AT), min(2 * (i - LN_AT) + 2, T + 1)):
                                    layer_norm(k)
                            if prep and 0 <= i - LN_AT - T // 2 - 1 < T // 2:
                                normalise_x(2 * (i - LN_AT - T // 2 - 1))
                                normalise_x(2 * (i - LN_AT - T // 2 - 1) + 1)
                        if prep:
                            if S0 + DOTS_AT <= i < S0 + DOTS_AT + T // 2:
                                token_dot(2 * (i - S0 - DOTS_AT))
                                token_dot(2 * (i - S0 - DOTS_AT) + 1)
                            if i == S0 + DOTS_AT + T // 2:
                                token_scores()
                            if S0 + RANK_AT <= i < S0 + RANK_AT + T:
                                rank(i - S0 - RANK_AT)
                    if main:
                        for j in jobs_at(NSTEP + LAG - 0.5, 999):
                            if j[1] == "out_proj" and j[2] == TC:
                                reciprocals(NG)
                                normalise_heads(prev + 1)
                            job(*j)
                    if prep:
                        commit()
            clear_semaphores()

        exact = nc.values_load(exact_flag[0:1, 0:1], min_val=0, max_val=1)
        turn(None, False, True, False, None)
        turn(0, True, True, False, x[1])
        with nc.Fori(1, B - 1) as b:
            turn(b, True, True, True, x[b + 1])
        turn(B - 1, True, False, True, None)


_INS = ["L0_attn_hidden_states", "L0_attn_Wq", "L0_attn_Wk", "L0_attn_Wv", "L0_attn_Wo",
        "L0_ffn_w1", "L0_ffn_b1", "L0_ffn_w2", "L0_ffn_b2"]


def kernel(**inputs):
    import numpy as _np
    import concourse.bacc as _bacc
    from concourse import mybir as _mybir
    from concourse.bass_utils import run_bass_kernel_spmd as _run

    nc = _bacc.Bacc("TRN2", target_bir_lowering=False, num_devices=1)
    arrays, args = {}, []
    for name in _INS:
        a = _np.ascontiguousarray(inputs[name])
        arrays[f"in_{name}"] = a
        args.append(nc.dram_tensor(f"in_{name}", a.shape, _mybir.dt.from_np(a.dtype), kind="ExternalInput").ap())
    shape = inputs["L0_attn_hidden_states"].shape
    args.append(nc.dram_tensor("out_y", shape, _mybir.dt.float32, kind="ExternalOutput").ap())
    kernel_program(nc, *args)
    r = _run(nc, [arrays], core_ids=[0])
    return r.results[0]["out_y"]
```

```python
from contextlib import ExitStack

import concourse.bass as bass
from concourse import mybir

F32 = mybir.dt.float32
F32R = mybir.dt.float32r
BF16 = mybir.dt.bfloat16
I32 = mybir.dt.int32
ALU = mybir.AluOpType
ACT = mybir.ActivationFunctionType
AX_X = mybir.AxisListType.X
RMAX = bass.bass_isa.ReduceOp.max

P = 128
WIN = 128
KEEP, ALPHA, HOPS = 0.33, 0.7, 2
NEG = 10000.0
LN_EPS, DIV_EPS = 1e-5, 1e-6
MASK_UNIT = 200.0
BOUND_MAX = 32.0
CH = 512
TC = CH // P


def kernel_program(nc, x, Wq, Wk, Wv, Wo, w1, b1, w2, b2, out):
    B, S, D = x.shape
    F = w1.shape[0]
    T = S // P
    NC = S // CH
    KD = D // P
    FT = F // P
    H, HD = 16, D // 16
    KVH = Wk.shape[1] // HD
    REP = H // KVH
    QT = H * HD // P
    HT = P // HD
    NQ = 4
    NPART = 6
    QPART = [0, 1, 2, 0, 1, 0]
    KPART = [0, 0, 0, 1, 1, 2]
    KROWS = NPART * HD
    SHIFT_ROWS = 3
    KEEPN = max(1, int(KEEP * S))
    VW = HD + 1
    assert (KD, QT, NC, T, KVH * HD) == (2, 2, 2, 8, P)

    STEPS = [(c, g, kb) for c in range(NC) for g in range(H // NQ) for kb in range(TC * (c + 1))]
    NSTEP = len(STEPS)
    NG = NC * H // NQ
    GROUP_END = [max(i for i, (c, g, _) in enumerate(STEPS) if c * (H // NQ) + g == n) for n in range(NG)]
    C1 = GROUP_END[H // NQ - 1] + 1
    NHID = 3
    LAG = 2

    def has_tri(i):
        return STEPS[i][2] >= TC * STEPS[i][0]

    def has_local(i):
        c, _, kb = STEPS[i]
        return TC * c <= kb + 1 < TC * (c + 1)

    def spans(i):
        c, _, kb = STEPS[i]
        lo = P * max(0, kb - TC * c)
        return lo, min(CH, max(lo, P * (kb + 2 - TC * c)))

    with ExitStack() as ctx:
        def sb(name, shape, dt=F32):
            return ctx.enter_context(nc.sbuf_tensor(name, shape, dt))

        def sem(name):
            s = ctx.enter_context(nc.semaphore(name))
            sems.append(s)
            return s

        sems = []
        ident = sb("ident", [P, P])
        ones = sb("ones", [P, P])
        before = sb("before", [P, P], BF16)
        after = sb("after", [P, P], BF16)
        band = sb("band", [P, 3, P], BF16)
        w1T = sb("w1T", [P, KD, F], F32R)
        w2T = sb("w2T", [P, FT, D], F32R)
        NW = 2 * D
        wqkv_hi = sb("wqkv_hi", [P, KD, NW], F32R)
        wqkv_lo = sb("wqkv_lo", [P, KD, NW], F32R)
        wo_sb = sb("wo_sb", [P, KD, D])
        b1_sb = sb("b1_sb", [P, FT])
        b2_bc = sb("b2_bc", [P, D])
        wsum = sb("wsum", [P, 2, T + 1])
        thr = sb("thr", [P, 2, 2])
        bound = sb("bound", [P, 8])
        shift = sb("shift", [P, 1])
        exact_flag = sb("exact_flag", [P, 1], I32)
        xn = sb("xn", [P, T, D])
        xT_hi = sb("xT_hi", [P, KD, S], F32R)
        xT_lo = sb("xT_lo", [P, KD, S], F32R)
        q_parts = sb("q_parts", [P, QT, 3, S], BF16)
        k_parts = sb("k_parts", [P, 3, S], BF16)
        q_stack = sb("q_stack", [P, H, S], BF16)
        k_stack = sb("k_stack", [P, KVH, S], BF16)
        v_sb = sb("v_sb", [P, T, KVH * VW + 32 - VW])
        probs = sb("probs", [P, 3, NQ, CH])
        near_mask = sb("near_mask", [P, T, P], BF16)
        mask_ident = sb("mask_ident", [P, P], BF16)
        key_bias = sb("key_bias", [P, T])
        landmark = sb("landmark", [P, T])
        hid = sb("hid", [P, NHID, CH])
        h_hi = sb("h_hi", [P, FT, CH], F32R)
        h_lo = sb("h_lo", [P, FT, CH], F32R)
        gate = sb("gate", [P, TC, D])
        mean_row = sb("mean_row", [P, D])
        att_raw = sb("att_raw", [P, CH])
        attT = sb("attT", [P, QT, CH])
        den = sb("den", [P, P])
        rden = den
        rden_bc = sb("rden_bc", [P, QT, CH])
        resid = sb("resid", [P, CH])
        stats = sb("stats", [P, T, 6])
        mv = sb("mv", [P, T, 2])
        root_in = sb("root_in", [P, T + 1])
        root = sb("root", [P, T + 1])
        root_t = sb("root_t", [P, T + 1])
        rstd = sb("rstd", [P, T])
        ssq = sb("ssq", [P, T + 1])
        norm = sb("norm", [P, T + 1])
        dots = sb("dots", [P, T])
        score = sb("score", [P, T])
        score_t = sb("score_t", [P, T])
        count = sb("count", [P, T, 4])
        lm_pad = sb("lm_pad", [P, T + 2], BF16)
        score_row = rden_bc[:, :, :].rearrange("p a n -> p (a n)")
        junk = resid[:, :].bitcast(BF16)
        w1_nat = probs[:, 0].rearrange("p a n -> p (a n)").rearrange("p (t d) -> p t d", d=D)
        w2_nat = probs[:, 1].rearrange("p a n -> p (a n)").rearrange("p (t f) -> p t f", f=F)
        x_prev = hid[:, :, :].rearrange("p a n -> p (a n)")[:, 0:TC * D].rearrange("p (t d) -> p t d", d=D)
        head_block = x_prev[:, 0, 0:P]
        w_tmp = probs[:, 2].rearrange("p a n -> p (a n)")
        scratch = q_parts[:, :, :, :].rearrange("p a b n -> p (a b n)").bitcast(F32)
        w_nat = scratch[:, 0:KD * NW].rearrange("p (k n) -> p k n", k=KD)
        wk_rep = scratch[:, KD * NW:KD * NW + KD * D].rearrange("p (k n) -> p k n", k=KD)
        gram = scratch[:, KD * (NW + D):KD * (NW + D) + D]

        sc_ps = ctx.enter_context(nc.psum_tensor("sc_ps", [P, 4, CH], F32))
        att_ps = ctx.enter_context(nc.psum_tensor("att_ps", [P, 2, CH], F32))
        aux_ps = ctx.enter_context(nc.psum_tensor("aux_ps", [P, 2, CH], F32))

        dve_chain, pool_chain = sem("dve_chain"), sem("pool_chain")
        w1_in, w2_in, wqkv_in, wo_in, b_in, x_in = (sem(n) for n in ("w1_in", "w2_in", "wqkv_in", "wo_in", "b_in", "x_in"))
        consts_done, wabs_done, wtotal_done, wT_done = (
            sem(n) for n in ("consts_done", "wabs_done", "wtotal_done", "wT_done"))
        wnat_split, gram_done, gram_sum_done, bound_sum_done, bound_ps_done, bound_max_done, bound_root_done = (
            sem(n) for n in ("wnat_split", "gram_done", "gram_sum_done", "bound_sum_done", "bound_ps_done",
                             "bound_max_done", "bound_root_done"))
        aux_done = sem("aux_done")
        aux_free = [sem("aux_free0"), sem("aux_free1")]
        aux_first = sem("aux_first")
        xn_done, xT_done = sem("xn_done"), sem("xT_done")
        dots_done, score_done, row_done, lm_done = (
            sem(n) for n in ("dots_done", "score_done", "row_done", "lm_done"))
        stack_in = [sem("stack_in0"), sem("stack_in1")]
        kstack_in, q_split = sem("kstack_in"), sem("q_split")
        sc_done, exp_done, pv_done = (sem(n) for n in ("sc_done", "exp_done", "pv_done"))
        att_out, att_in, rden_done, rden_in, attT_done = (
            sem(n) for n in ("att_out", "att_in", "rden_done", "rden_in", "attT_done"))
        hid_split, hi_done, hid_split_pool, z_done, gate_done, prod_done, y_done, xres_in, y_out = (
            sem(n) for n in ("hid_split", "hi_done", "hid_split_pool", "z_done", "gate_done", "prod_done", "y_done", "xres_in", "y_out"))
        xprev_in, w_first = sem("xprev_in"), sem("w_first")

        index_done, masked_done, max_done, max_row_done, max_split, max_in = (
            sem(n) for n in ("index_done", "masked_done", "max_done", "max_row_done", "max_split", "max_in"))

        def link(eng, chain, counter):
            def f(ins):
                counter[0] += 1
                ins.then_inc(chain, 1)
                eng.wait_ge(chain, counter[0])
            return f

        def clear_semaphores():
            with nc.Block(no_gpsimd_drain=True) as block:
                @block.sync
                def _(sp):
                    lo = min(s.num for s in sems)
                    assert [s.num for s in sems] == list(range(lo, lo + len(sems)))
                    sp.sem_clear(range(lo, lo + len(sems)))

        def rsqrt(dve, lk, m):
            v, y, t = root_in[:, 0:m], root[:, 0:m], root_t[:, 0:m]
            lk(dve.tensor_scalar(y.bitcast(I32), v.bitcast(I32), -0.5, 1597463007.0, ALU.mult, ALU.add))
            lk(dve.tensor_scalar(v, v, -0.5, None, ALU.mult))
            for _ in range(3):
                lk(dve.tensor_tensor(t, v, y, ALU.mult))
                lk(dve.tensor_tensor(t, t, y, ALU.mult))
                lk(dve.scalar_tensor_tensor(y, t, 1.5, y, ALU.add, ALU.mult))

        def layer_norm(dve, lk, k):
            if k < T:
                dve.bn_stats(stats[:, k, :], xn[:, k, :])
                lk(dve.bn_stats(stats[:, k + 1, :], xn[:, k + 1, :]))
                dve.bn_aggr(mv[:, k, :], stats[:, k, :])
                lk(dve.bn_aggr(mv[:, k + 1, :], stats[:, k + 1, :]))
            else:
                lk(dve.tensor_scalar(root_in[:, 0:T], mv[:, :, 1], LN_EPS, None, ALU.add))
                rsqrt(dve, lk, T)
                lk(dve.tensor_copy(rstd[:, :], root[:, 0:T]))

        def w_columns(lo):
            src, parts = w_nat[:, :, lo:lo + P], [w[:, :, lo:lo + P] for w in (wqkv_hi, wqkv_lo)]
            if lo < D + P:
                src = src.rearrange("p k (h d) -> p k h d", d=HD)
                parts = [w.rearrange("p k (d h) -> p k h d", d=HD) for w in parts]
            return src, parts

        with nc.Block(no_gpsimd_drain=True) as block:
            @block.sync
            def _(sp):
                sp.dma_start(w1_nat, w1.rearrange("(t p) d -> p t d", p=P)).then_inc(w1_in, 16)
                sp.dma_start(w2_nat, w2.rearrange("(t p) f -> p t f", p=P)).then_inc(w2_in, 16)
                sp.dma_start(b1_sb[:, :], b1.rearrange("(t p) -> p t", p=P), allow_slow_non_contiguous=True).then_inc(b_in, 16)
                sp.dma_start(b2_bc[0:1, :], b2.rearrange("(a n) -> a n", a=1)).then_inc(b_in, 16)
                sp.wait_ge(b_in, 32)
                sp.wait_ge(x_in, 16)

            @block.scalar
            def _(act):
                act.dma_start(w_nat[:, :, 0:D], Wq.rearrange("(k p) n -> p k n", p=P)).then_inc(wqkv_in, 16)
                act.dma_start(w_nat[:, :, D:D + P], Wk.rearrange("(k p) n -> p k n", p=P)).then_inc(wqkv_in, 16)
                act.dma_start(w_nat[:, :, D + P:NW], Wv.rearrange("(k p) n -> p k n", p=P)).then_inc(wqkv_in, 16)
                act.dma_start(wo_sb[:, :, :], Wo.rearrange("(k p) n -> p k n", p=P)).then_inc(wo_in, 16)
                act.dma_start(xn[:, :, :], x[0].rearrange("(t p) d -> p t d", p=P)).then_inc(x_in, 16)
                act.wait_ge(wqkv_in, 48)
                for lo in range(0, NW, P):
                    src, (hi, _) = w_columns(lo)
                    act.activation(hi, src, ACT.Copy).then_inc(w_first, 1)
                for n in range(2 * KD * FT // TC):
                    act.wait_ge(wT_done, n + 1)
                    src = sc_ps[:, n, :] if n < 4 else (att_ps[:, n - 4, :] if n < 6 else aux_ps[:, n - 6, :])
                    if n < 4:
                        dst = w1T[:, n // 2, (n % 2) * CH:(n % 2 + 1) * CH]
                    else:
                        dst = w2T[:, 2 * (n - 4):2 * (n - 3), :].rearrange("p t d -> p (t d)")
                    act.activation(dst, src, ACT.Copy)
                act.wait_ge(bound_max_done, 2)
                act.activation(bound[:, 5:6], bound[:, 4:5], ACT.Sqrt).then_inc(bound_root_done, 1)
                act.wait_ge(wo_in, 16)

            @block.gpsimd
            def _(pool):
                lk = link(pool, pool_chain, [0])
                for t, v in ((ident, 0.0), (ones, 1.0), (before, 1.0), (after, 1.0), (hid, 1.0),
                             (band, 1.0), (mask_ident, 0.0), (v_sb, 0.0), (lm_pad, 0.0), (count, 0.0), (den, 1.0)):
                    last = pool.memset(t[tuple(slice(None) for _ in t.shape)], v)
                lk(last)

                def select(m, pattern, op, base, mult, fill):
                    lk(pool.affine_select(out=m, in_=m, compare_op=op, fill=fill, base=base,
                                          pattern=pattern, channel_multiplier=mult))
                select(ident[:, :], [[-1, P]], ALU.not_equal, 0, 1, 1.0)
                select(before[:, :], [[-1, P]], ALU.is_gt, 0, 1, 0.0)
                select(after[:, :], [[1, P]], ALU.is_gt, 0, -1, 0.0)
                select(mask_ident[:, :], [[-1, P]], ALU.not_equal, 0, 1, -MASK_UNIT)
                hb = head_block.rearrange("p (g d) -> p g d", d=HD)
                select(hb, [[-HD, HT], [0, HD]], ALU.is_ge, 0, 1, 0.0)
                select(hb, [[HD, HT], [0, HD]], ALU.is_ge, HD - 1, -1, 0.0)
                select(band[:, 0, :], [[-1, P]], ALU.is_ge, HOPS - P, 1, 0.0)
                select(band[:, 1, :], [[-1, P]], ALU.is_ge, HOPS, 1, 0.0)
                select(band[:, 1, :], [[1, P]], ALU.is_ge, HOPS, -1, 0.0)
                select(band[:, 2, :], [[1, P]], ALU.is_ge, HOPS - P, -1, 0.0)
                pool.wait_ge(b_in, 32)
                pool.partition_broadcast(b2_bc[:, :], b2_bc[0:1, :]).then_inc(consts_done, 1)
                lk(pool.memset(v_sb[:, :, 0:KVH * VW].rearrange("p t (j w) -> p t j w", w=VW)[:, :, :, HD:VW], 1.0))
                lk(pool.memset(q_stack[KROWS:KROWS + 32, :, :].bitcast(F32), 0.0))
                lk(pool.memset(k_stack[KROWS:KROWS + 32, :, :], 1.0))
                pool.wait_ge(bound_sum_done, 1)
                lk(pool.partition_all_reduce(bound[:, 2:4], bound[:, 0:2], P, RMAX))
                pool.sem_inc(bound_max_done, 1)

            @block.vector
            def _(dve):
                lk = link(dve, dve_chain, [0])
                for n, (nat, s) in enumerate(((w1_nat, w1_in), (w2_nat, w2_in))):
                    dve.wait_ge(s, 16)
                    v = nat if n == 0 else nat.rearrange("p t f -> p (t f)").rearrange("p (t d) -> p t d", d=D)
                    lk(dve.tensor_reduce(wsum[:, n, 0:T], v, AX_X, ALU.add, apply_absolute_value=True))
                    dve.tensor_reduce(wsum[:, n, T:T + 1], wsum[:, n, 0:T], AX_X, ALU.add).then_inc(wabs_done, 1)
                dve.wait_ge(w_first, NW // P)
                for lo in range(0, NW, P):
                    src, (hi, low) = w_columns(lo)
                    dve.tensor_tensor(low, src, hi.bitcast(F32), ALU.subtract)
                for k in range(KD):
                    for r in range(REP):
                        last = dve.tensor_copy(wk_rep[:, k, :].rearrange("p (j r d) -> p j r d", j=KVH, r=REP)[:, :, r, :],
                                               w_nat[:, k, D:D + P].rearrange("p (j d) -> p j d", j=KVH))
                last.then_inc(wnat_split, 1)
                dve.wait_ge(wtotal_done, 1)
                lk(dve.tensor_scalar(thr[:, :, 0], aux_ps[:, 0, 0:2], 1.0 / (F * D), 0.7, ALU.mult, ALU.mult))
                lk(dve.tensor_scalar(thr[:, :, 1], thr[:, :, 0], -1.0, None, ALU.mult))
                for n, nat in enumerate((w1_nat, w2_nat)):
                    flat = nat.rearrange("p a n -> p (a n)")
                    lk(dve.tensor_scalar(w_tmp, flat, thr[:, n, 1:2], None, ALU.is_le))
                    ins = dve.scalar_tensor_tensor(flat, flat, thr[:, n, 0:1], w_tmp, ALU.is_ge, ALU.subtract)
                    ins.then_inc(wabs_done, 1)
                    dve.wait_ge(wabs_done, 3 + n)
                dve.wait_ge(x_in, 16)
                for k in range(0, T, 2):
                    layer_norm(dve, lk, k)
                dve.wait_ge(gram_done, 1)
                lk(dve.tensor_copy(gram, aux_ps[:, 1, 0:D]))
                lk(dve.tensor_tensor(gram, gram, aux_ps[:, 1, D:2 * D], ALU.mult))
                for m in range(QT):
                    lk(dve.tensor_tensor(gram[:, m * P:(m + 1) * P], gram[:, m * P:(m + 1) * P], head_block, ALU.mult))
                dve.tensor_reduce(bound[:, 6:8], gram.rearrange("p (m n) -> p m n", n=P), AX_X, ALU.add).then_inc(gram_sum_done, 1)
                dve.wait_ge(bound_ps_done, 1)
                dve.tensor_copy(bound[:, 0:2], aux_ps[:, 0, 8:10]).then_inc(bound_sum_done, 1)
                layer_norm(dve, lk, T)
                dve.wait_ge(bound_max_done, 1)
                dve.tensor_reduce(bound[:, 4:5], bound[:, 2:4], AX_X, ALU.max).then_inc(bound_max_done, 1)
                dve.wait_ge(bound_root_done, 1)
                lk(dve.tensor_scalar(bound[:, 6:7], bound[:, 5:6], 1.001 * D / HD ** 0.5, None, ALU.mult))
                lk(dve.tensor_scalar(bound[:, 7:8], bound[:, 6:7], BOUND_MAX, None, ALU.is_le))
                lk(dve.tensor_scalar(exact_flag[:, :], bound[:, 7:8], -1.0, 1.0, ALU.mult, ALU.add))
                lk(dve.tensor_scalar(bound[:, 6:7], bound[:, 6:7], BOUND_MAX, -1.0, ALU.min, ALU.mult))
                lk(dve.tensor_tensor(shift[:, :], bound[:, 6:7], bound[:, 7:8], ALU.mult))

            @block.tensor
            def _(pe):
                pe.wait_ge(consts_done, 1)
                pe.wait_ge(wabs_done, 2)
                pe.matmul(aux_ps[:, 0, 0:2], ones[:, :], wsum[:, :, T], start=True, stop=True).then_inc(wtotal_done, 1)
                pe.wait_ge(wnat_split, 1)
                for n, w in enumerate((w_nat, wk_rep)):
                    for m in range(QT):
                        for k in range(KD):
                            last = pe.matmul(aux_ps[:, 1, (QT * n + m) * P:(QT * n + m + 1) * P], w[:, k, m * P:(m + 1) * P],
                                             w[:, k, m * P:(m + 1) * P], start=(k == 0), stop=(k == KD - 1))
                last.then_inc(gram_done, 1)
                for n in range(2 * KD * FT // TC):
                    if n in (0, 4):
                        pe.wait_ge(wabs_done, 3 + n // 4)
                    if n == 6:
                        pe.wait_ge(gram_sum_done, 1)
                        pe.matmul(aux_ps[:, 0, 8:10], head_block, bound[:, 6:8], start=True, stop=True).then_inc(bound_ps_done, 1)
                        pe.wait_ge(bound_sum_done, 1)
                    dst = sc_ps[:, n, :] if n < 4 else (att_ps[:, n - 4, :] if n < 6 else aux_ps[:, n - 6, :])
                    for q in range(TC):
                        if n < 4:
                            src = w1_nat[:, (n % 2) * TC + q, (n // 2) * P:(n // 2 + 1) * P]
                        else:
                            f = 2 * (n - 4) + q // 2
                            src = w2_nat[:, q % 2, f * P:(f + 1) * P]
                        last = pe.transpose(dst[:, q * P:(q + 1) * P], src, ident[:, :])
                    last.then_inc(wT_done, 1)
        clear_semaphores()

        def row_maxima():
            flat = [probs[:, i].rearrange("p a n -> p (a n)") for i in range(3)]
            key_at, mask = flat[0][:, 0:S], flat[0][:, S:2 * S]
            masked, landmark_row = flat[1][:, 0:S], flat[1][:, S:2 * S]
            row_max, query_at, behind = flat[2][:, 0:H], flat[2][:, H:H + 1], flat[2][:, H + 1:H + 2]
            left = flat[2][0:H, P:2 * P]
            parts = flat[2][0:H, 2 * P:4 * P].bitcast(BF16)[:, 0:3 * P].rearrange("h (r n) -> h r n", r=3)

            with nc.Block(no_gpsimd_drain=True) as block:
                @block.sync
                def _(sp):
                    for i in range(NPART):
                        for m in range(QT):
                            sp.dma_start(q_stack[i * HD:(i + 1) * HD, m * HT:(m + 1) * HT, CH:S],
                                         q_parts[:, m, QPART[i], CH:S]).then_inc(stack_in[1], 16)
                    sp.wait_ge(stack_in[1], 16 * NPART * QT)
                    sp.wait_ge(index_done, 2)

                @block.gpsimd
                def _(pool):
                    for at, n, step in ((key_at, S, 0), (query_at, 1, 1)):
                        pool.iota(at, [[1, n]], base=0, channel_multiplier=step,
                                  allow_small_or_imprecise_dtypes=True).then_inc(index_done, 1)

                @block.tensor
                def _(pe):
                    for t in range(T):
                        last = pe.transpose(sc_ps[:, t // TC, (t % TC) * P:(t % TC + 1) * P],
                                            landmark[:, t:t + 1].to_broadcast([P, P]), ident[:, :])
                    last.then_inc(row_done, 1)

                @block.vector
                def _(dve):
                    dve.memset(q_stack[KROWS:P, :, :], 0.0)

                @block.scalar
                def _(act):
                    act.wait_ge(row_done, 1)
                    act.activation(landmark_row, sc_ps[:, 0:NC, :].rearrange("p a n -> p (a n)"), ACT.Copy)
            clear_semaphores()

            with nc.Fori(0, T) as t:
                with nc.Block(no_gpsimd_drain=True) as block:
                    @block.tensor
                    def _(pe):
                        for h in range(H):
                            if h >= 2:
                                pe.wait_ge(masked_done, h - 1)
                            for half in range(NC):
                                last = pe.matmul(sc_ps[:, 2 * (h % 2) + half, :], q_stack[:, h, bass.ds(t * P, P)],
                                                 k_stack[:, h // REP, half * CH:(half + 1) * CH], start=True, stop=True)
                            last.then_inc(sc_done, 1)
                        pe.wait_ge(max_done, 1)
                        pe.transpose(aux_ps[0:H, 0, 0:P], row_max, ident[:, :]).then_inc(max_row_done, 1)

                    @block.vector
                    def _(dve):
                        lk = link(dve, dve_chain, [0])
                        lk(dve.tensor_scalar(behind, query_at, -float(WIN), None, ALU.add))
                        lk(dve.scalar_tensor_tensor(mask, key_at, behind, landmark_row, ALU.is_gt, ALU.max))
                        lk(dve.scalar_tensor_tensor(mask, key_at, query_at, mask, ALU.is_le, ALU.mult))
                        lk(dve.tensor_scalar(mask, mask, -1.0, NEG * HD ** 0.5, ALU.add, ALU.mult))
                        for h in range(H):
                            dve.wait_ge(sc_done, h + 1)
                            ps = sc_ps[:, 2 * (h % 2):2 * (h % 2) + 2, :].rearrange("p a n -> p (a n)")
                            dve.tensor_tensor(masked, ps, mask, ALU.add).then_inc(masked_done, 1)
                            dve.wait_ge(masked_done, h + 1)
                            lk(dve.tensor_reduce(row_max[:, h:h + 1], masked, AX_X, ALU.max))
                        dve.tensor_scalar(row_max, row_max, -1.0, None, ALU.mult).then_inc(max_done, 1)
                        lk(dve.tensor_scalar(query_at, query_at, float(P), None, ALU.add))
                        dve.wait_ge(aux_first, 1)
                        lk(dve.tensor_tensor(left, aux_ps[0:H, 0, 0:P], parts[:, 0, :], ALU.subtract))
                        lk(dve.tensor_copy(parts[:, 1, :], left))
                        dve.tensor_tensor(parts[:, 2, :], left, parts[:, 1, :], ALU.subtract).then_inc(max_split, 1)

                    @block.scalar
                    def _(act):
                        act.wait_ge(max_row_done, 1)
                        act.activation(parts[:, 0, :], aux_ps[0:H, 0, 0:P], ACT.Copy).then_inc(aux_first, 1)

                    @block.sync
                    def _(sp):
                        sp.wait_ge(max_split, 1)
                        for r in range(SHIFT_ROWS):
                            sp.dma_start(q_stack[KROWS + r:KROWS + r + 1, :, bass.ds(t * P, P)],
                                         parts[:, r, :]).then_inc(max_in, 16)
                        sp.wait_ge(max_in, 16 * SHIFT_ROWS)
                clear_semaphores()

        FFN_DOWN_AT = (6, 7, 8, 9, 10, 11, 12, 13)
        DOTS_AT, RANK_AT = 6, 19
        LN_AT = 5

        def jobs_of(main, prep, prev):
            jobs = []
            n_prev = TC if prev else 0
            if prev:
                jobs += [(4 + t // 2, "out_proj", TC + t, t) for t in range(TC)]
            if main:
                jobs += [(at, "ffn_down", i // 2, i % 2) for i, at in enumerate(FFN_DOWN_AT)]
                jobs += [(C1 - 0.5, "ffn_up", 1, f, f) for f in range(FT)]
                jobs += [(C1 + at, "out_proj", t, n_prev + t) for t, at in enumerate((11, 13, 15, 16))]
                jobs += [(C1 + 18 + 2 * t + half, "ffn_down", TC + t, half) for t in range(TC) for half in range(2)]
            if main and not prep:
                jobs += [(NSTEP + 5, "out_proj", TC + t, n_prev + TC + t) for t in range(TC)]
            if prep:
                s = C1 if main else 0
                s1 = C1 if main else -7
                at = (s, s, s + 1, s + 2) if main else (1, 2, 3, 4)
                jobs += [(s, "mean_row")]
                jobs += [(at[KD * c + k], "transpose", k, c) for c in range(NC) for k in range(KD)]
                jobs += [(s + 5 + c, "k_proj", c) for c in range(NC)]
                jobs += [(s + at, "q_proj", m, c) for (m, c), at in zip(((0, 0), (1, 0), (0, 1), (1, 1)),
                                                                         (6, 8, 10, 12) if main else (7, 8, 9, 10))]
                jobs += [(s1 + 17, "score_row", i) for i in range(2)]
                jobs += [(s1 + 28, "dilate")]
                if main:
                    jobs += [(NSTEP + 3, "v_proj", i) for i in range(2)]
                    jobs += [(NSTEP + (0 if f < 2 else LAG), "ffn_up", 0, f, FT + f) for f in range(FT)]
                else:
                    jobs += [(12, "v_proj", i) for i in range(2)]
                    jobs += [(16 + f // 2, "ffn_up", 0, f, f) for f in range(FT)]
            return sorted(jobs, key=lambda j: j[0])

        def turn(b, main, prep, prev, x_next):
            if main:
                with nc.If(exact != 0):
                    row_maxima()
            jobs = jobs_of(main, prep, prev)
            n_prev = TC if prev else 0
            norms = [(0, (0, 1))] * prev + [(NG // 2, (0, 1))]
            if not prep:
                norms += [(NG - H // NQ // 2, (0,)), (NG, (1,))]
            spread_by = [16 * TC * sum(len(ms) for _, ms in norms[:n + 1]) for n in range(len(norms))]
            own = int(prev)
            S1 = C1 if main else -7
            last_step = 23

            def jobs_at(lo, hi):
                return [(n,) + j[1:] for n, j in enumerate(jobs) if lo <= j[0] < hi]

            bank_of, used = [], [0, 0]
            for j in jobs:
                if j[1] == "ffn_down" and j[3]:
                    bank_of.append(bank_of[-1])
                    continue
                bank = sum(used) % 2
                bank_of.append((bank, used[bank]))
                used[bank] += 1

            n_transposes = [n for n, j in enumerate(jobs) if j[1] == "transpose"]

            with nc.Block(no_gpsimd_drain=True) as block:
                @block.sync
                def _(sp):
                    def stack_q(c):
                        cs = slice(c * CH, (c + 1) * CH)
                        for i in range(NPART):
                            for m in range(QT):
                                sp.dma_start(q_stack[i * HD:(i + 1) * HD, m * HT:(m + 1) * HT, cs],
                                             q_parts[:, m, QPART[i], cs]).then_inc(stack_in[c], 16)

                    def stack_k():
                        for i in range(NPART):
                            sp.dma_start(k_stack[i * HD:(i + 1) * HD, :, :], k_parts[:, KPART[i], :]).then_inc(kstack_in, 16)

                    def att_group(n):
                        c, g = n // (H // NQ), n % (H // NQ)
                        sp.wait_ge(att_out, n + 1)
                        if g == 0 and (c == 1 or prev):
                            sp.wait_ge(aux_done, 1 + [i for i, j in enumerate(jobs) if j[1] == "out_proj"][n_prev - 1 + c * TC])
                        h = g * NQ
                        for q in range(NQ):
                            row = (h % HT + q) * HD
                            sp.dma_start(attT[row:row + HD, h // HT, :], att_raw[32 * q:32 * q + HD, :]).then_inc(att_in, 16)
                        sp.dma_start(den[h * TC:(h + NQ) * TC, :], att_raw[HD:P:32, :]).then_inc(att_in, 16)

                    def spread_rden(n):
                        sp.wait_ge(rden_done, n + 1)
                        for m in norms[n][1]:
                            for s in range(TC):
                                src = rden[m * HT * TC + s:(m + 1) * HT * TC:TC, :]
                                sp.dma_start(rden_bc[:, m, s * P:(s + 1) * P],
                                             src.unsqueeze(1).to_broadcast([HT, HD, P])).then_inc(rden_in, 16)

                    if main:
                        xb = x[b].rearrange("(t p) d -> p t d", p=P)
                        ob = out[b].rearrange("(t p) d -> p t d", p=P)
                        if prev:
                            xp = x[b - 1].rearrange("(t p) d -> p t d", p=P)
                            op = out[b - 1].rearrange("(t p) d -> p t d", p=P)
                            spread_rden(0)
                            sp.dma_start(x_prev[:, :, :], xp[:, TC:T, :]).then_inc(xprev_in, 16)
                        if prep:
                            sp.dma_start(xn[:, :, :], x_next.rearrange("(t p) d -> p t d", p=P)).then_inc(x_in, 16)
                        stack_q(1)
                        if prev:
                            sp.wait_ge(y_done, TC)
                            sp.dma_start(op[:, TC:T, :], x_prev[:, :, :]).then_inc(y_out, 16)
                        for n in range(4):
                            att_group(n)
                        spread_rden(own)
                        x_end = TC if prep else T
                        if prep:
                            sp.wait_ge(aux_done, n_transposes[-1] + 1)
                            sp.wait_ge(dots_done, T)
                        sp.dma_start(xn[:, 0:x_end, :], xb[:, 0:x_end, :]).then_inc(xres_in, 16)
                        att_group(4)
                        if prep:
                            sp.wait_ge(q_split, 2)
                            stack_q(0)
                        att_group(5)
                        if not prep:
                            spread_rden(own + 1)
                        sp.wait_ge(y_done, n_prev + TC)
                        sp.dma_start(ob[:, 0:TC, :], xn[:, 0:TC, :]).then_inc(y_out, 16)
                        att_group(6)
                        if prep:
                            sp.wait_ge(sc_done, 2 * NSTEP)
                            stack_k()
                        att_group(7)
                        if prep:
                            sp.wait_ge(att_in, 16 * (NQ + 1) * NG)
                        else:
                            spread_rden(own + 2)
                            for t in range(TC, T, 2):
                                sp.wait_ge(y_done, n_prev + t + 2)
                                sp.dma_start(ob[:, t:t + 2, :], xn[:, t:t + 2, :]).then_inc(y_out, 16)
                        sp.wait_ge(y_out, 16 * (prev + 1 + (0 if prep else TC // 2)))
                    else:
                        sp.wait_ge(q_split, QT * NC)
                        stack_k()
                        stack_q(0)
                    if prep:
                        sp.wait_ge(hid_split_pool, (1 + main) * FT // 2)
                        sp.wait_ge(stack_in[0], 16 * NPART * QT)
                        sp.wait_ge(kstack_in, 16 * NPART)

                @block.tensor
                def _(pe):
                    def job(n, kind, *a):
                        bank, before_it = bank_of[n]
                        ps = aux_ps[:, bank, :]
                        if before_it and not (kind == "ffn_down" and a[1]):
                            pe.wait_ge(aux_free[bank], before_it)
                        if kind == "ffn_up":
                            c, f, _ = a
                            for k in range(KD):
                                for part in (xT_hi, xT_lo):
                                    last = pe.matmul(ps, w1T[:, k, f * P:(f + 1) * P], part[:, k, c * CH:(c + 1) * CH],
                                                     start=(k == 0 and part is xT_hi), stop=(k == KD - 1 and part is xT_lo))
                        elif kind == "ffn_down":
                            t, half = a
                            if t >= TC:
                                pe.wait_ge(hid_split, FT // 2)
                                pe.wait_ge(hid_split_pool, FT // 2)
                            q = t % TC
                            for f in range(half * FT // 2, (half + 1) * FT // 2):
                                for part in (h_hi, h_lo):
                                    last = pe.matmul(ps[:, 0:D], part[:, f, q * P:(q + 1) * P], w2T[:, f, :],
                                                     start=(f == 0 and part is h_hi), stop=(f == FT - 1 and part is h_lo))
                        elif kind == "out_proj":
                            t, u = a
                            q = t % TC
                            for k in range(KD):
                                pe.wait_ge(attT_done, u // TC + 1 + (k if u >= n_prev + TC else 0))
                                last = pe.matmul(ps[:, 0:D], attT[:, k, q * P:(q + 1) * P], wo_sb[:, k, :],
                                                 start=(k == 0), stop=(k == KD - 1))
                        elif kind == "transpose":
                            k, c = a
                            pe.wait_ge(xn_done, TC * (c + 1))
                            for q in range(TC):
                                last = pe.transpose(ps[:, q * P:(q + 1) * P], xn[:, c * TC + q, k * P:(k + 1) * P], ident[:, :])
                        elif kind in ("k_proj", "q_proj"):
                            m, c = a if kind == "q_proj" else (QT, a[0])
                            pe.wait_ge(xT_done, KD * NC)
                            ws, xs = slice(m * P, (m + 1) * P), slice(c * CH, (c + 1) * CH)
                            mms = [(w, xp, k) for k in range(KD) for w, xp in ((wqkv_hi, xT_hi), (wqkv_hi, xT_lo), (wqkv_lo, xT_hi))]
                            for i, (w, xp, k) in enumerate(mms):
                                last = pe.matmul(ps, w[:, k, ws], xp[:, k, xs], start=(i == 0), stop=(i == len(mms) - 1))
                        elif kind == "v_proj":
                            for q in range(TC):
                                t = a[0] * TC + q
                                mms = [(xp, w, k) for k in range(KD) for xp, w in ((xT_hi, wqkv_hi), (xT_lo, wqkv_hi), (xT_hi, wqkv_lo))]
                                for i, (xp, w, k) in enumerate(mms):
                                    last = pe.matmul(ps[:, q * P:(q + 1) * P], xp[:, k, t * P:(t + 1) * P], w[:, k, D + P:NW],
                                                     start=(i == 0), stop=(i == len(mms) - 1))
                        elif kind == "mean_row":
                            pe.wait_ge(xn_done, T)
                            for t in range(T):
                                last = pe.matmul(ps[:, 0:D], ones[:, :], xn[:, t, :], start=(t == 0), stop=(t == T - 1))
                        elif kind == "score_row":
                            pe.wait_ge(score_done, 1)
                            for q in range(TC):
                                t = a[0] * TC + q
                                last = pe.transpose(ps[:, q * P:(q + 1) * P], score[:, t:t + 1].to_broadcast([P, P]), ident[:, :])
                        elif kind == "dilate":
                            pe.wait_ge(lm_done, 1)
                            for i in range(3):
                                last = pe.matmul(ps[:, 0:T], band[:, i, :], lm_pad[:, i:i + T], start=(i == 0), stop=(i == 2))
                        last.then_inc(aux_done, 1)

                    def scores(i, u):
                        c, g, kb = STEPS[i]
                        if i == C1 and u == 0:
                            pe.wait_ge(stack_in[1], 16 * NPART * QT)
                        lo, near = spans(i)
                        if i >= 1:
                            pe.wait_ge(exp_done, 2 * (i - 1) + u + 1)
                        for hh in range(2):
                            h = g * NQ + 2 * u + hh
                            last = pe.matmul(sc_ps[:, 2 * u + hh, lo:CH], k_stack[0:KROWS + SHIFT_ROWS, h // REP, kb * P:(kb + 1) * P],
                                             q_stack[0:KROWS + SHIFT_ROWS, h, c * CH + lo:(c + 1) * CH], start=True, stop=(near == lo))
                        if near > lo:
                            first = 0 if has_tri(i) else kb + 1
                            end = kb + 2 if has_local(i) else 1
                            for hh in range(2):
                                last = pe.matmul(sc_ps[:, 2 * u + hh, lo:near], mask_ident[:, :], near_mask[:, first:end:kb + 1, :],
                                                 start=False, stop=True)
                        last.then_inc(sc_done, 1)

                    def values(i):
                        c, g, kb = STEPS[i]
                        n = c * (H // NQ) + g
                        if kb == 0 and n >= 2:
                            pe.wait_ge(att_out, n - 1)
                        pe.wait_ge(exp_done, 2 * (i + 1))
                        lo = spans(i)[0]
                        for q in range(NQ):
                            j = (g * NQ + q) // REP
                            last = pe.matmul(att_ps[32 * q:32 * q + 32, n % 2, lo:CH], v_sb[:, kb, j * VW:j * VW + 32],
                                             probs[:, i % 3, q, lo:CH], start=(kb == 0), stop=(kb == TC * (c + 1) - 1))
                        last.then_inc(pv_done, 1)

                    if main:
                        for i in range(NSTEP + LAG):
                            for j in jobs_at(i - 0.5, i):
                                job(*j)
                            if i < NSTEP:
                                scores(i, 0)
                            if i >= LAG:
                                values(i - LAG)
                            if i < NSTEP:
                                scores(i, 1)
                            for j in jobs_at(i, i + 0.5):
                                job(*j)
                        for j in jobs_at(NSTEP + LAG - 0.5, 999):
                            job(*j)
                    else:
                        for j in jobs_at(0, 999):
                            job(*j)

                @block.scalar
                def _(act):
                    def job(n, kind, *a):
                        bank, before_it = bank_of[n]
                        ps = aux_ps[:, bank, :]
                        if kind == "ffn_up":
                            c, f, u = a
                            act.wait_ge(aux_done, n + 1)
                            if u >= NHID:
                                act.wait_ge([hid_split, hid_split_pool][(u - NHID) % 2], (u - NHID) // 2 + 1)
                            if u == 0 and prev:
                                act.wait_ge(y_out, 16)
                            act.activation(hid[:, u % NHID, :], ps, ACT.Gelu, bias=b1_sb[:, f:f + 1]).then_inc(aux_free[bank], 1)
                        elif kind == "transpose" and not main:
                            k, c = a
                            act.wait_ge(aux_done, n + 1)
                            act.activation(xT_hi[:, k, c * CH:(c + 1) * CH], ps, ACT.Copy).then_inc(aux_first, 1)
                        elif kind in ("k_proj", "q_proj"):
                            dst = k_parts[:, 0, a[0] * CH:(a[0] + 1) * CH] if kind == "k_proj" else \
                                q_parts[:, a[0], 0, a[1] * CH:(a[1] + 1) * CH]
                            act.wait_ge(aux_done, n + 1)
                            if main and kind == "q_proj":
                                act.wait_ge(stack_in[1], 16 * NPART * QT)
                            act.activation(dst, ps, ACT.Copy).then_inc(aux_first, 1)
                        elif kind == "v_proj":
                            act.wait_ge(aux_done, n + 1)
                            for q in range(TC):
                                t = a[0] * TC + q
                                last = act.activation(v_sb[:, t, 0:KVH * VW].rearrange("p (j w) -> p j w", w=VW)[:, :, 0:HD],
                                                      ps[:, q * P:(q + 1) * P].rearrange("p (j d) -> p j d", d=HD), ACT.Copy)
                            last.then_inc(aux_free[bank], 1)
                        elif kind == "score_row":
                            act.wait_ge(aux_done, n + 1)
                            act.activation(score_row[:, a[0] * CH:(a[0] + 1) * CH], ps, ACT.Copy).then_inc(row_done, 1)
                            act.wait_ge(row_done, a[0] + 1)
                            act.sem_inc(aux_free[bank], 1)

                    def gates(c):
                        act.wait_ge(z_done, TC * (c + 1))
                        act.activation(gate[:, :, :], gate[:, :, :], ACT.Silu).then_inc(gate_done, 1)

                    def exps(i):
                        c, g, kb = STEPS[i]
                        lo, near = spans(i)
                        if i >= 3:
                            act.wait_ge(pv_done, i - 2)
                        for u in range(2):
                            act.wait_ge(sc_done, 2 * i + u + 1)
                            us = slice(2 * u, 2 * u + 2)
                            if near > lo:
                                last = act.activation(probs[:, i % 3, us, lo:near], sc_ps[:, us, lo:near], ACT.Exp,
                                                      bias=shift[:, 0:1], scale=HD ** -0.5)
                            if near < CH:
                                last = act.activation(probs[:, i % 3, us, near:CH], sc_ps[:, us, near:CH], ACT.Exp,
                                                      bias=key_bias[:, kb:kb + 1], scale=HD ** -0.5)
                            last.then_inc(exp_done, 1)

                    for i in range(NSTEP if main else last_step + 1):
                        for j in jobs_at(i - 0.5, i):
                            job(*j)
                        if main and i == C1:
                            gates(0)
                        if main:
                            exps(i)
                        for j in jobs_at(i, i + 0.5):
                            job(*j)
                    if main:
                        tail = jobs_at(NSTEP - 0.5, 999)
                        first = [j for j in tail if j[1] == "ffn_up"]
                        for j in first:
                            job(*j)
                        gates(1)
                        for j in tail[len(first):]:
                            job(*j)

                @block.gpsimd
                def _(pool):
                    def residual(t, u):
                        if u == 0 and prev:
                            pool.wait_ge(xprev_in, 16)
                        if u == n_prev:
                            pool.wait_ge(xres_in, 16)
                        pool.wait_ge(prod_done, u + 1)
                        x_tile = x_prev[:, t - TC, :] if u < n_prev else xn[:, t, :]
                        pool.tensor_tensor(x_tile, x_tile, gate[:, t % TC, :], ALU.add).then_inc(y_done, 1)

                    def split_rest(f, u):
                        pool.wait_ge(hi_done, u // 2 + 1)
                        pool.tensor_tensor(h_lo[:, f, :], hid[:, u % NHID, :], h_hi[:, f, :].bitcast(F32),
                                           ALU.subtract).then_inc(hid_split_pool, 1)

                    for _, kind, *a in jobs_at(0, 999):
                        if kind == "out_proj":
                            residual(*a)
                        if kind == "ffn_up" and a[2] % 2:
                            split_rest(*a[1:])

                @block.vector
                def _(dve):
                    lk = link(dve, dve_chain, [0])

                    def commit():
                        lk(dve.tensor_scalar(key_bias[:, :], landmark[:, :], -1.0, NEG, ALU.add, ALU.mult))
                        lk(dve.tensor_scalar(key_bias[:, :], key_bias[:, :], shift[:, 0:1], None, ALU.add))
                        lk(dve.tensor_scalar(near_mask[:, 0, :], before[:, :], MASK_UNIT, None, ALU.mult))
                        for t in range(T - 1):
                            last = dve.tensor_scalar(near_mask[:, t + 1, :], before[:, :], landmark[:, t:t + 1], -MASK_UNIT, ALU.max, ALU.mult)
                        lk(last)
                        dve.tensor_scalar(near_mask[:, 1:T, :], near_mask[:, 1:T, :], MASK_UNIT, None, ALU.add)

                    def job(n, kind, *a):
                        bank, before_it = bank_of[n]
                        ps = aux_ps[:, bank, :]
                        if kind == "ffn_up":
                            c, f, u = a
                            dve.wait_ge(aux_free[bank], before_it + 1)
                            whole = hid[:, u % NHID, :]
                            ins = dve.tensor_copy(h_hi[:, f, :], whole)
                            if u % 2:
                                ins.then_inc(hi_done, 1)
                            else:
                                lk(ins)
                                dve.tensor_tensor(h_lo[:, f, :], whole, h_hi[:, f, :].bitcast(F32), ALU.subtract).then_inc(hid_split, 1)
                        elif kind == "ffn_down" and a[1]:
                            t = a[0]
                            dve.wait_ge(aux_done, n + 1)
                            if prev or t >= TC:
                                dve.wait_ge(y_done, t + 1 - (0 if prev else TC))
                            dve.tensor_tensor(gate[:, t % TC, :], ps[:, 0:D], b2_bc[:, :], ALU.add).then_inc(z_done, 1)
                            dve.wait_ge(z_done, t + 1)
                            dve.sem_inc(aux_free[bank], 1)
                        elif kind == "out_proj":
                            t, u = a
                            dve.wait_ge(aux_done, n + 1)
                            if u >= n_prev and t % TC == 0:
                                dve.wait_ge(gate_done, t // TC + 1)
                            dve.tensor_tensor(gate[:, t % TC, :], ps[:, 0:D], gate[:, t % TC, :], ALU.mult).then_inc(prod_done, 1)
                            dve.wait_ge(prod_done, u + 1)
                            dve.sem_inc(aux_free[bank], 1)
                        elif kind == "transpose":
                            k, c = a
                            m = c * KD + k
                            if main:
                                dve.wait_ge(aux_done, n + 1)
                                dve.tensor_copy(xT_hi[:, k, c * CH:(c + 1) * CH], ps).then_inc(aux_first, 1)
                            dve.wait_ge(aux_first, m + 1)
                            dve.tensor_tensor(xT_lo[:, k, c * CH:(c + 1) * CH], ps,
                                              xT_hi[:, k, c * CH:(c + 1) * CH].bitcast(F32), ALU.subtract).then_inc(xT_done, 1)
                            dve.wait_ge(xT_done, m + 1)
                            dve.sem_inc(aux_free[bank], 1)
                        elif kind in ("k_proj", "q_proj"):
                            first = KD * NC + (a[0] if kind == "k_proj" else NC + a[1] * QT + a[0])
                            c = a[0] if kind == "k_proj" else a[1]
                            part = [(k_parts[:, r, c * CH:(c + 1) * CH] if kind == "k_proj" else
                                     q_parts[:, a[0], r, c * CH:(c + 1) * CH]) for r in range(3)]
                            dve.wait_ge(aux_first, first + 1)
                            ins = dve.tensor_tensor(resid[:, :], ps, part[0], ALU.subtract)
                            ins.then_inc(aux_free[bank], 1)
                            dve.wait_ge(aux_free[bank], before_it + 1)
                            lk(dve.tensor_copy(part[1], resid[:, :]))
                            ins = dve.tensor_tensor(part[2], resid[:, :], part[1], ALU.subtract)
                            if kind == "q_proj":
                                ins.then_inc(q_split, 1)
                                dve.wait_ge(q_split, 1 + QT * c + a[0])
                            else:
                                lk(ins)
                        elif kind == "mean_row":
                            dve.wait_ge(aux_done, n + 1)
                            dve.tensor_scalar(mean_row[:, :], ps[:, 0:D], 1.0 / S, None, ALU.mult).then_inc(aux_free[bank], 1)
                            dve.wait_ge(aux_free[bank], before_it + 1)
                        elif kind == "dilate":
                            dve.wait_ge(aux_done, n + 1)
                            dve.tensor_scalar(landmark[:, :], ps[:, 0:T], 1.0, None, ALU.min).then_inc(aux_free[bank], 1)
                            dve.wait_ge(aux_free[bank], before_it + 1)

                    def normalise_x(t):
                        for k in (t, t + 1):
                            dve.tensor_scalar(xn[:, k, :], xn[:, k, :], mv[:, k, 0:1], rstd[:, k:k + 1], ALU.subtract, ALU.mult).then_inc(xn_done, 1)
                        dve.wait_ge(xn_done, t + 2)
                        for k in (t, t + 1):
                            last = dve.scalar_tensor_tensor(resid[:, (k - t) * D:(k - t + 1) * D], xn[:, k, :], 1.0, xn[:, k, :],
                                                            ALU.mult, ALU.mult, accum_out=ssq[:, k:k + 1])
                        lk(last)

                    def token_dots(t):
                        for k in (t, t + 1):
                            dve.scalar_tensor_tensor(resid[:, (k - t) * D:(k - t + 1) * D], xn[:, k, :], 1.0, mean_row[:, :],
                                                     ALU.mult, ALU.mult, accum_out=dots[:, k:k + 1]).then_inc(dots_done, 1)
                        dve.wait_ge(dots_done, t + 2)

                    def token_scores():
                        lk(dve.scalar_tensor_tensor(resid[:, 0:D], mean_row[:, :], 1.0, mean_row[:, :], ALU.mult, ALU.mult,
                                                    accum_out=ssq[:, T:T + 1]))
                        lk(dve.tensor_copy(root_in[:, :], ssq[:, :]))
                        rsqrt(dve, lk, T + 1)
                        lk(dve.tensor_tensor(norm[:, :], ssq[:, :], root[:, :], ALU.mult))
                        lk(dve.tensor_scalar(root_t[:, 0:T], norm[:, 0:T], norm[:, T:T + 1], DIV_EPS, ALU.mult, ALU.add))
                        lk(dve.reciprocal(root_t[:, 0:T], root_t[:, 0:T]))
                        lk(dve.tensor_tensor(score_t[:, :], dots[:, :], root_t[:, 0:T], ALU.mult))
                        lk(dve.tensor_scalar(score_t[:, :], score_t[:, :], -(1.0 - ALPHA), None, ALU.mult))
                        lk(dve.tensor_scalar(score[:, :], norm[:, 0:T], ALPHA, None, ALU.mult))
                        dve.tensor_tensor(score[:, :], score[:, :], score_t[:, :], ALU.add).then_inc(score_done, 1)

                    def rank(t):
                        if t == 0:
                            dve.wait_ge(score_done, 1)
                            dve.wait_ge(row_done, 2)
                        own, at = score[:, t:t + 1], slice(t * P, (t + 1) * P)
                        if t > 0:
                            dve.tensor_scalar(junk[:, 0:t * P], score_row[:, 0:t * P], own, 0.0, ALU.is_ge, ALU.add,
                                              accum_out=count[:, t, 0:1])
                        if t < T - 1:
                            dve.tensor_scalar(junk[:, (t + 1) * P:S], score_row[:, (t + 1) * P:S], own, 0.0, ALU.is_gt, ALU.add,
                                              accum_out=count[:, t, 1:2])
                        lk(dve.scalar_tensor_tensor(junk[:, at], score_row[:, at], own, before[:, :], ALU.is_ge, ALU.mult,
                                                    accum_out=count[:, t, 2:3]))
                        lk(dve.scalar_tensor_tensor(junk[:, at], score_row[:, at], own, after[:, :], ALU.is_gt, ALU.mult,
                                                    accum_out=count[:, t, 3:4]))
                        if t == T - 1:
                            lk(dve.tensor_reduce(score_t[:, :], count[:, :, :], AX_X, ALU.add))
                            dve.tensor_scalar(lm_pad[:, 1:T + 1], score_t[:, :], float(KEEPN), None, ALU.is_lt).then_inc(lm_done, 1)

                    def group_out(n):
                        dve.wait_ge(pv_done, GROUP_END[n] + 1)
                        if n >= 1:
                            dve.wait_ge(att_in, 16 * (NQ + 1) * n)
                        dve.tensor_copy(att_raw[:, :], att_ps[:, n % 2, :]).then_inc(att_out, 1)

                    def reciprocals(n):
                        groups, ms = norms[n]
                        if groups:
                            dve.wait_ge(att_in, 16 * (NQ + 1) * groups)
                        rows = slice(ms[0] * HT * TC, (ms[-1] + 1) * HT * TC)
                        dve.reciprocal(rden[rows, :], den[rows, :]).then_inc(rden_done, 1)

                    def normalise_heads(n):
                        dve.wait_ge(rden_in, spread_by[n])
                        ms = slice(norms[n][1][0], norms[n][1][-1] + 1)
                        dve.tensor_tensor(attT[:, ms, :], attT[:, ms, :], rden_bc[:, ms, :], ALU.mult).then_inc(attT_done, 1)

                    if prev:
                        reciprocals(0)
                    if prep and not main:
                        for k in range(0, T, 2):
                            normalise_x(k)
                    for i in range(last_step + 1 if not main else NSTEP + LAG):
                        for j in jobs_at(i - 0.5, i):
                            job(*j)
                        for j in jobs_at(i, i + 0.5):
                            job(*j)
                        if main:
                            for n in range(NG):
                                if GROUP_END[n] + LAG == i:
                                    group_out(n)
                            if prev and i == 3:
                                normalise_heads(0)
                            if i == C1 + 5:
                                reciprocals(own)
                            if i == C1 + 8:
                                normalise_heads(own)
                            if not prep and i == GROUP_END[5] + LAG + 4:
                                reciprocals(own + 1)
                            if not prep and i == GROUP_END[5] + LAG + 7:
                                normalise_heads(own + 1)
                            if prep and LN_AT <= i < LN_AT + T // 2 + 1:
                                if i == LN_AT:
                                    dve.wait_ge(x_in, 16)
                                layer_norm(dve, lk, 2 * (i - LN_AT))
                            if prep and 0 <= i - LN_AT - T // 2 - 1 < T // 2:
                                normalise_x(2 * (i - LN_AT - T // 2 - 1))
                        if prep:
                            dots_at = C1 + DOTS_AT if main else 0
                            if dots_at <= i < dots_at + T // 2:
                                token_dots(2 * (i - dots_at))
                            if i == dots_at + T // 2:
                                token_scores()
                            if S1 + RANK_AT <= i < S1 + RANK_AT + T:
                                rank(i - S1 - RANK_AT)
                    if main:
                        for j in jobs_at(NSTEP + LAG - 0.5, 999):
                            if j[1] == "out_proj" and j[2] == TC:
                                reciprocals(own + 2)
                                normalise_heads(own + 2)
                            job(*j)
                    if prep:
                        commit()
            clear_semaphores()

        exact = nc.values_load(exact_flag[0:1, 0:1], min_val=0, max_val=1)
        turn(None, False, True, False, None)
        turn(0, True, True, False, x[1])
        with nc.Fori(1, B - 1) as b:
            turn(b, True, True, True, x[b + 1])
        turn(B - 1, True, False, True, None)


_INS = ["L0_attn_hidden_states", "L0_attn_Wq", "L0_attn_Wk", "L0_attn_Wv", "L0_attn_Wo",
        "L0_ffn_w1", "L0_ffn_b1", "L0_ffn_w2", "L0_ffn_b2"]


def kernel(**inputs):
    import numpy as _np
    import concourse.bacc as _bacc
    from concourse import mybir as _mybir
    from concourse.bass_utils import run_bass_kernel_spmd as _run

    nc = _bacc.Bacc("TRN2", target_bir_lowering=False, num_devices=1)
    arrays, args = {}, []
    for name in _INS:
        a = _np.ascontiguousarray(inputs[name])
        arrays[f"in_{name}"] = a
        args.append(nc.dram_tensor(f"in_{name}", a.shape, _mybir.dt.from_np(a.dtype), kind="ExternalInput").ap())
    shape = inputs["L0_attn_hidden_states"].shape
    args.append(nc.dram_tensor("out_y", shape, _mybir.dt.float32, kind="ExternalOutput").ap())
    kernel_program(nc, *args)
    r = _run(nc, [arrays], core_ids=[0])
    return r.results[0]["out_y"]
```
